# Optimizing a Trainium2 kernel written in Bass

```python
import numpy as np
import jax
import jax.numpy as jnp

def _softmax(x, axis=-1):
    return jax.nn.softmax(x, axis=axis)

def _gelu(x):
    return jax.nn.gelu(x, approximate=True)

def _silu(x):
    return jax.nn.silu(x)

def _sigmoid(x):
    return jax.nn.sigmoid(x)

def _layernorm(x, axis=-1, eps=1e-05):
    m = jnp.mean(x, axis=axis, keepdims=True)
    v = jnp.var(x, axis=axis, keepdims=True)
    return (x - m) / jnp.sqrt(v + eps)

def _scatter_add(tgt, idx, src, axis=0):
    return tgt.at[idx].add(src)

def _segment_sum(src, seg, n):
    return jax.ops.segment_sum(src, seg, n)
kernel_name = 'mk_gnn_preln_d2_gnn_r8_a2ec07'

def setup_inputs(seed: int=0):
    np.random.seed(seed)
    _w = jnp.asarray

    def _rec_inputs():
        import jax
        import jax.numpy as jnp
        _gk = jax.random.key(seed)
        x = 8.953e-05 + 1 * jax.random.normal(jax.random.fold_in(_gk, 1), (12500, 32), jnp.float32)
        src = jax.random.randint(jax.random.fold_in(_gk, 2), (200000,), 0, 12500, jnp.int32)
        dst = jax.random.randint(jax.random.fold_in(_gk, 3), (200000,), 0, 12500, jnp.int32)
        _o = jnp.argsort(dst, stable=True)
        src = src[_o]
        dst = dst[_o]
        edge_attr_3 = 0.000844983 + 0.999762 * jax.random.normal(jax.random.fold_in(_gk, 11), (200000, 3), jnp.float32)
        edge_weight = jax.random.uniform(jax.random.fold_in(_gk, 13), (200000,), jnp.float32, 0.0, 1)
        return (x, src, dst, edge_attr_3, edge_weight)
    x, src, dst, edge_attr_3, edge_weight = _rec_inputs()

    def _L0_gnn_setup():
        import jax, jax.numpy as jnp
        import numpy as np
        from math import factorial, pi, sqrt
        MUL = 8
        RS = [(MUL, 0), (MUL, 1)]
        N_NODES = 2500
        N_EDGES = 80000
        FEAT_DIM = sum((m * (2 * l + 1) for m, l in RS))
        R_DIM = sum((mo * mi * (2 * min(lo, li) + 1) for mo, lo in RS for mi, li in RS))
        HIDDEN = 64

        def _cg(j1, j2, j3, m1, m2, m3):
            if m1 + m2 != m3:
                return 0.0
            f = factorial
            pre = sqrt((2 * j3 + 1) * f(j3 + j1 - j2) * f(j3 - j1 + j2) * f(j1 + j2 - j3) / f(j1 + j2 + j3 + 1))
            pre *= sqrt(f(j3 + m3) * f(j3 - m3) * f(j1 - m1) * f(j1 + m1) * f(j2 - m2) * f(j2 + m2))
            kmin = max(0, j2 - j3 - m1, j1 - j3 + m2)
            kmax = min(j1 + j2 - j3, j1 - m1, j2 + m2)
            s = 0.0
            for k in range(kmin, kmax + 1):
                s += (-1) ** k / (f(k) * f(j1 + j2 - j3 - k) * f(j1 - m1 - k) * f(j2 + m2 - k) * f(j3 - j2 + m1 + k) * f(j3 - j1 - m2 + k))
            return pre * s

        def _w3j_complex(l1, l2, l3):
            w = np.zeros((2 * l1 + 1, 2 * l2 + 1, 2 * l3 + 1))
            for m1 in range(-l1, l1 + 1):
                for m2 in range(-l2, l2 + 1):
                    m3 = -(m1 + m2)
                    if abs(m3) <= l3:
                        w[m1 + l1, m2 + l2, m3 + l3] = (-1) ** (l1 - l2 - m3) / sqrt(2 * l3 + 1) * _cg(l1, l2, l3, m1, m2, -m3)
            return w

        def _A(l):
            A = np.zeros((2 * l + 1, 2 * l + 1), dtype=complex)
            A[l, l] = 1.0
            for m in range(1, l + 1):
                A[l + m, l + m] = (-1) ** m / sqrt(2)
                A[l + m, l - m] = 1.0 / sqrt(2)
                A[l - m, l - m] = 1j / sqrt(2)
                A[l - m, l + m] = -1j * (-1) ** m / sqrt(2)
            return A

        def real_w3j(l1, l2, l3):
            wc = _w3j_complex(l1, l2, l3).astype(complex)
            wr = np.einsum('abc,ma,nb,oc->mno', wc, _A(l1).conj(), _A(l2).conj(), _A(l3).conj())
            i = int(np.argmax(np.abs(wr)))
            ph = wr.flat[i] / abs(wr.flat[i])
            wr = wr / ph
            assert np.abs(wr.imag).max() < 1e-10
            return np.real(wr).astype(np.float32)
        _W3J = {}
        for _mo, _lo in RS:
            for _mi, _li in RS:
                for _lf in range(abs(_lo - _li), _lo + _li + 1):
                    if (_lo, _lf, _li) not in _W3J:
                        _W3J[_lo, _lf, _li] = jnp.asarray(real_w3j(_lo, _lf, _li))
        _NORM = []
        for _mo, _lo in RS:
            _num = sum((mi * (2 * min(_lo, li) + 1) for mi, li in RS))
            _NORM.append(sqrt(4.0 * pi) * sqrt(2.0 * _lo + 1.0) / sqrt(_num))
        _F_OFFS = [0] + list(np.cumsum([mi * (2 * li + 1) for mi, li in RS]))

        def spherical_harmonics(rel_vec):
            r = rel_vec / jnp.linalg.norm(rel_vec, axis=-1, keepdims=True)
            x, y, z = (r[:, 0], r[:, 1], r[:, 2])
            y0 = jnp.full_like(x, 0.5 / sqrt(pi))[:, None]
            c1 = sqrt(3.0 / (4.0 * pi))
            y1 = c1 * jnp.stack([y, z, x], axis=-1)
            c2a = 0.5 * sqrt(15.0 / pi)
            c2b = 0.25 * sqrt(5.0 / pi)
            c2c = 0.25 * sqrt(15.0 / pi)
            y2 = jnp.stack([c2a * x * y, c2a * y * z, c2b * (3.0 * z * z - 1.0), c2a * x * z, c2c * (x * x - y * y)], axis=-1)
            return jnp.concatenate([y0, y1, y2], axis=-1)
        key = jax.random.key(seed)
        ks = jax.random.split(key, 6)
        features = jax.random.normal(ks[0], (N_NODES, FEAT_DIM), dtype=jnp.float32)
        abs_distances = jax.random.uniform(ks[1], (N_EDGES,), dtype=jnp.float32, minval=0.1, maxval=1.0)
        rel_vec = jax.random.normal(ks[2], (N_EDGES, 3), dtype=jnp.float32)
        edge_index = jax.random.randint(ks[3], (2, N_EDGES), 0, N_NODES, dtype=jnp.int32)
        w1 = jax.random.normal(ks[4], (1, HIDDEN), dtype=jnp.float32)
        b1 = jnp.zeros((HIDDEN,), jnp.float32)
        w2 = jax.random.normal(ks[5], (HIDDEN, R_DIM), dtype=jnp.float32) / sqrt(HIDDEN)
        b2 = jnp.zeros((R_DIM,), jnp.float32)
        return {'features': features, 'abs_distances': abs_distances, 'rel_vec': rel_vec, 'edge_index': edge_index, 'w1': w1, 'b1': b1, 'w2': w2, 'b2': b2}
    _L0_gnn_all = _L0_gnn_setup()
    _L0_gnn_in = {k: v for k, v in _L0_gnn_all.items() if k in ('w1', 'b1', 'w2', 'b2')}
    del _L0_gnn_all

    def _L1_gnn_setup():
        import jax, jax.numpy as jnp
        import numpy as np
        N_NODES = 12500
        N_EDGES = 200000
        IN_F = 32
        HID = 128

        def _gcn_norm(edge_index, n_nodes):
            loops = jnp.arange(n_nodes, dtype=edge_index.dtype)
            src = jnp.concatenate([edge_index[0], loops])
            dst = jnp.concatenate([edge_index[1], loops])
            ones = jnp.ones(src.shape[0], dtype=jnp.float32)
            deg = jax.ops.segment_sum(ones, dst, num_segments=n_nodes)
            deg_inv_sqrt = jnp.where(deg > 0, jax.lax.rsqrt(deg), 0.0)
            norm = deg_inv_sqrt[src] * deg_inv_sqrt[dst]
            return (src, dst, norm)

        def _gcn_conv(x, src, dst, norm, W, b, n_nodes):
            h = x @ W
            msg = h[src] * norm[:, None]
            out = jax.ops.segment_sum(msg, dst, num_segments=n_nodes)
            return out + b
        key = jax.random.key(seed)
        ks = jax.random.split(key, 8)
        x = jax.random.normal(ks[0], (N_NODES, IN_F), dtype=jnp.float32)
        edge_index = jax.random.randint(ks[1], (2, N_EDGES), 0, N_NODES, dtype=jnp.int64)
        W1 = jax.random.normal(ks[2], (IN_F, HID), dtype=jnp.float32) / np.sqrt(IN_F)
        b1 = jnp.zeros((HID,), dtype=jnp.float32)
        W2 = jax.random.normal(ks[3], (HID, HID), dtype=jnp.float32) / np.sqrt(HID)
        b2 = jnp.zeros((HID,), dtype=jnp.float32)
        W3 = jax.random.normal(ks[4], (HID, IN_F), dtype=jnp.float32) / np.sqrt(HID)
        b3 = jnp.zeros((IN_F,), dtype=jnp.float32)
        return {'x': x, 'edge_index': edge_index, 'W1': W1, 'b1': b1, 'W2': W2, 'b2': b2, 'W3': W3, 'b3': b3}
    _L1_gnn_all = _L1_gnn_setup()
    _L1_gnn_in = {k: v for k, v in _L1_gnn_all.items() if k in ('W1', 'b1', 'W2', 'b2', 'W3', 'b3')}
    del _L1_gnn_all
    return {'x': x, 'src': src, 'dst': dst, 'edge_attr_3': edge_attr_3, 'edge_weight': edge_weight, 'L0_gnn_w1': _L0_gnn_in['w1'], 'L0_gnn_b1': _L0_gnn_in['b1'], 'L0_gnn_w2': _L0_gnn_in['w2'], 'L0_gnn_b2': _L0_gnn_in['b2'], 'L1_gnn_W1': _L1_gnn_in['W1'], 'L1_gnn_b1': _L1_gnn_in['b1'], 'L1_gnn_W2': _L1_gnn_in['W2'], 'L1_gnn_b2': _L1_gnn_in['b2'], 'L1_gnn_W3': _L1_gnn_in['W3'], 'L1_gnn_b3': _L1_gnn_in['b3']}

def reference(x, src, dst, edge_attr_3, edge_weight, L0_gnn_w1, L0_gnn_b1, L0_gnn_w2, L0_gnn_b2, L1_gnn_W1, L1_gnn_b1, L1_gnn_W2, L1_gnn_b2, L1_gnn_W3, L1_gnn_b3):
    import jax
    import jax.numpy as jnp

    def _L0_gnn_ref(features, abs_distances, rel_vec, edge_index, w1, b1, w2, b2):
        import jax, jax.numpy as jnp
        import numpy as np
        from math import factorial, pi, sqrt
        MUL = 8
        RS = [(MUL, 0), (MUL, 1)]
        N_NODES = 2500
        N_EDGES = 80000
        FEAT_DIM = sum((m * (2 * l + 1) for m, l in RS))
        R_DIM = sum((mo * mi * (2 * min(lo, li) + 1) for mo, lo in RS for mi, li in RS))
        HIDDEN = 64

        def _cg(j1, j2, j3, m1, m2, m3):
            if m1 + m2 != m3:
                return 0.0
            f = factorial
            pre = sqrt((2 * j3 + 1) * f(j3 + j1 - j2) * f(j3 - j1 + j2) * f(j1 + j2 - j3) / f(j1 + j2 + j3 + 1))
            pre *= sqrt(f(j3 + m3) * f(j3 - m3) * f(j1 - m1) * f(j1 + m1) * f(j2 - m2) * f(j2 + m2))
            kmin = max(0, j2 - j3 - m1, j1 - j3 + m2)
            kmax = min(j1 + j2 - j3, j1 - m1, j2 + m2)
            s = 0.0
            for k in range(kmin, kmax + 1):
                s += (-1) ** k / (f(k) * f(j1 + j2 - j3 - k) * f(j1 - m1 - k) * f(j2 + m2 - k) * f(j3 - j2 + m1 + k) * f(j3 - j1 - m2 + k))
            return pre * s

        def _w3j_complex(l1, l2, l3):
            w = np.zeros((2 * l1 + 1, 2 * l2 + 1, 2 * l3 + 1))
            for m1 in range(-l1, l1 + 1):
                for m2 in range(-l2, l2 + 1):
                    m3 = -(m1 + m2)
                    if abs(m3) <= l3:
                        w[m1 + l1, m2 + l2, m3 + l3] = (-1) ** (l1 - l2 - m3) / sqrt(2 * l3 + 1) * _cg(l1, l2, l3, m1, m2, -m3)
            return w

        def _A(l):
            A = np.zeros((2 * l + 1, 2 * l + 1), dtype=complex)
            A[l, l] = 1.0
            for m in range(1, l + 1):
                A[l + m, l + m] = (-1) ** m / sqrt(2)
                A[l + m, l - m] = 1.0 / sqrt(2)
                A[l - m, l - m] = 1j / sqrt(2)
                A[l - m, l + m] = -1j * (-1) ** m / sqrt(2)
            return A

        def real_w3j(l1, l2, l3):
            wc = _w3j_complex(l1, l2, l3).astype(complex)
            wr = np.einsum('abc,ma,nb,oc->mno', wc, _A(l1).conj(), _A(l2).conj(), _A(l3).conj())
            i = int(np.argmax(np.abs(wr)))
            ph = wr.flat[i] / abs(wr.flat[i])
            wr = wr / ph
            assert np.abs(wr.imag).max() < 1e-10
            return np.real(wr).astype(np.float32)
        _W3J = {}
        for _mo, _lo in RS:
            for _mi, _li in RS:
                for _lf in range(abs(_lo - _li), _lo + _li + 1):
                    if (_lo, _lf, _li) not in _W3J:
                        _W3J[_lo, _lf, _li] = jnp.asarray(real_w3j(_lo, _lf, _li))
        _NORM = []
        for _mo, _lo in RS:
            _num = sum((mi * (2 * min(_lo, li) + 1) for mi, li in RS))
            _NORM.append(sqrt(4.0 * pi) * sqrt(2.0 * _lo + 1.0) / sqrt(_num))
        _F_OFFS = [0] + list(np.cumsum([mi * (2 * li + 1) for mi, li in RS]))

        def spherical_harmonics(rel_vec):
            r = rel_vec / jnp.linalg.norm(rel_vec, axis=-1, keepdims=True)
            x, y, z = (r[:, 0], r[:, 1], r[:, 2])
            y0 = jnp.full_like(x, 0.5 / sqrt(pi))[:, None]
            c1 = sqrt(3.0 / (4.0 * pi))
            y1 = c1 * jnp.stack([y, z, x], axis=-1)
            c2a = 0.5 * sqrt(15.0 / pi)
            c2b = 0.25 * sqrt(5.0 / pi)
            c2c = 0.25 * sqrt(15.0 / pi)
            y2 = jnp.stack([c2a * x * y, c2a * y * z, c2b * (3.0 * z * z - 1.0), c2a * x * z, c2c * (x * x - y * y)], axis=-1)
            return jnp.concatenate([y0, y1, y2], axis=-1)
        src, dst = (edge_index[0], edge_index[1])
        R = jax.nn.relu(abs_distances[:, None] @ w1 + b1) @ w2 + b2
        Y = spherical_harmonics(rel_vec)
        Fj = features[src]
        E = Fj.shape[0]
        msg_blocks = []
        r_off = 0
        for i, (mo, lo) in enumerate(RS):
            acc = jnp.zeros((E, mo, 2 * lo + 1), dtype=features.dtype)
            for j, (mi, li) in enumerate(RS):
                n_lf = 2 * min(lo, li) + 1
                sz = mo * mi * n_lf
                Rb = R[:, r_off:r_off + sz].reshape(E, mo, mi, n_lf)
                r_off += sz
                Fb = Fj[:, _F_OFFS[j]:_F_OFFS[j + 1]].reshape(E, mi, 2 * li + 1)
                for k, lf in enumerate(range(abs(lo - li), lo + li + 1)):
                    C = _W3J[lo, lf, li]
                    Yf = Y[:, lf * lf:(lf + 1) * (lf + 1)]
                    acc = acc + _NORM[i] * jnp.einsum('euv,ef,evi,ofi->euo', Rb[..., k], Yf, Fb, C)
            msg_blocks.append(acc.reshape(E, -1))
        msg = jnp.concatenate(msg_blocks, axis=-1)
        out = jnp.zeros((features.shape[0], msg.shape[1]), dtype=features.dtype)
        out = out.at[dst].add(msg)
        return out

    def _L1_gnn_ref(x, edge_index, W1, b1, W2, b2, W3, b3):
        import jax, jax.numpy as jnp
        import numpy as np
        N_NODES = 12500
        N_EDGES = 200000
        IN_F = 32
        HID = 128

        def _gcn_norm(edge_index, n_nodes):
            loops = jnp.arange(n_nodes, dtype=edge_index.dtype)
            src = jnp.concatenate([edge_index[0], loops])
            dst = jnp.concatenate([edge_index[1], loops])
            ones = jnp.ones(src.shape[0], dtype=jnp.float32)
            deg = jax.ops.segment_sum(ones, dst, num_segments=n_nodes)
            deg_inv_sqrt = jnp.where(deg > 0, jax.lax.rsqrt(deg), 0.0)
            norm = deg_inv_sqrt[src] * deg_inv_sqrt[dst]
            return (src, dst, norm)

        def _gcn_conv(x, src, dst, norm, W, b, n_nodes):
            h = x @ W
            msg = h[src] * norm[:, None]
            out = jax.ops.segment_sum(msg, dst, num_segments=n_nodes)
            return out + b
        n = x.shape[0]
        src, dst, norm = _gcn_norm(edge_index, n)
        h = jax.nn.relu(_gcn_conv(x, src, dst, norm, W1, b1, n))
        h = jax.nn.relu(_gcn_conv(h, src, dst, norm, W2, b2, n))
        h = jax.nn.relu(_gcn_conv(h, src, dst, norm, W3, b3, n))
        return h
    edge_index = jnp.stack([src, dst])
    h = jnp.maximum(_layernorm(x, axis=-1), 0.0)
    x = x + _L0_gnn_ref(h, edge_weight, edge_attr_3, edge_index, L0_gnn_w1, L0_gnn_b1, L0_gnn_w2, L0_gnn_b2)
    h = jnp.maximum(_layernorm(x, axis=-1), 0.0)
    x = x + _L1_gnn_ref(h, edge_index, L1_gnn_W1, L1_gnn_b1, L1_gnn_W2, L1_gnn_b2, L1_gnn_W3, L1_gnn_b3)
    return x

_drawn_inputs = setup_inputs


def setup_inputs(seed=0):
    import zlib

    import numpy as np

    out = dict(_drawn_inputs(seed))
    spreads = {'L0_gnn_b1': (0.0, 0.1),
     'L0_gnn_b2': (0.0, 0.1),
     'L1_gnn_b1': (0.0, 0.661),
     'L1_gnn_b2': (0.0, 0.385),
     'L1_gnn_b3': (0.0, 0.286)}
    factors = {}
    for name, (base, spread) in spreads.items():
        noise = np.random.default_rng([zlib.crc32(name.encode()), seed]).standard_normal(out[name].shape)
        drawn = base * np.exp(spread * noise) if base else spread * noise
        out[name] = jnp.asarray(drawn.astype(out[name].dtype))
    for name, factor in factors.items():
        out[name] = (out[name] * factor).astype(out[name].dtype)
    return out
```

```python
import concourse.bass as bass
from concourse import mybir
from contextlib import ExitStack
from math import pi, sqrt

P = 128
N = 12500
E = 200000
F = 32
MUL = 8
NB = -(-N // P)
NPAD = NB * P
NTAIL = N - (NB - 1) * P
TPG = 8
GE = TPG * P
NG = -(-E // GE)
UNROLL = 4
NIT = NG // UNROLL
ETAIL = E - (NG - 1) * GE
PTAIL = ETAIL // TPG
WIN = 128
RDIM = 6 * MUL * MUL
HID0 = 64
HID = 128
NLAYER = 4
WIDTH = [F, F, HID, F]
EPS = 1e-5
SEGW = MUL + 1 + 24 * 16
assert NG % UNROLL == 0 and PTAIL * TPG == ETAIL

NORM0 = sqrt(4 * pi) / sqrt(2 * MUL)
NORM1 = sqrt(4 * pi) * sqrt(3) / sqrt(4 * MUL)
Y0 = 0.5 / sqrt(pi)
Y1 = sqrt(3 / (4 * pi))
K00 = NORM0 * Y0
K01 = NORM0 * Y1 / sqrt(3)
K10 = NORM1 * Y1 / sqrt(3)
K11_0 = NORM1 * Y0 / sqrt(3)
K11_1 = NORM1 * Y1 / sqrt(6)
K11_2 = NORM1 * sqrt(3 / (8 * pi))

fp32 = mybir.dt.float32
i32 = mybir.dt.int32
ALU = mybir.AluOpType
ACT = mybir.ActivationFunctionType
X = mybir.AxisListType.X


def gnn_kernel(nc, x, src, dst, edge_attr, edge_weight, w1, b1, w2, b2,
               W1, B1, W2, B2, W3, B3, out):
    ctx = ExitStack()
    with ctx:
        def sb(name, shape, dt=fp32):
            return ctx.enter_context(nc.sbuf_tensor(name, shape, dt))

        def pb(name, shape, dt=fp32):
            return ctx.enter_context(nc.psum_tensor(name, shape, dt))

        def sem(name):
            return ctx.enter_context(nc.semaphore(name))

        tables = [nc.dram_tensor(f"table{n}", [NPAD, WIDTH[n]], fp32, kind="Internal").ap()
                  for n in range(NLAYER)]
        meta_d = nc.dram_tensor("meta_d", [NG, 2], i32, kind="Internal").ap()

        accT = sb("accT", [P, NPAD + WIN])
        arena = sb("arena", [P, NPAD])
        direction = arena[:, 0:NG * TPG * 5].rearrange("p (t c) -> p t c", c=5)
        norm_row = arena[:, :]
        xn = sb("xn", [P, NB, F])
        scratch = sb("scratch", [P, 2 * NB * F])
        msg = scratch[:, 0:2 * 4 * 401].rearrange("p (h t c) -> p h t c", h=2, t=4)
        prodA = scratch[:, 3208:3208 + 2 * 4 * 256].rearrange("p (h t c) -> p h t c", h=2, t=4)
        lnA = scratch[:, 0:NB * F].rearrange("p (b f) -> p b f", f=F)
        lnB = scratch[:, NB * F:2 * NB * F].rearrange("p (b f) -> p b f", f=F)
        ybuf = scratch[:, 0:1024].rearrange("p (s n) -> p s n", s=2)
        rbuf = scratch[:, 1024:2048].rearrange("p (s n) -> p s n", s=2)
        tbuf = scratch[:, 2048:3072].rearrange("p (s n) -> p s n", s=2)
        squares = scratch[:, 0:NG * TPG * 3].rearrange("p (t c) -> p t c", c=3)
        length = scratch[:, NG * TPG * 3:NG * TPG * 4]
        dst_rows = accT[0:NB, 0:2 * GE].bitcast(i32).rearrange("p (h e) -> p h e", h=2)
        dst_i = accT[:, 2048:2048 + NG * TPG].bitcast(i32)
        attr = accT[:, 4096:4096 + NG * TPG * 3].rearrange("p (t c) -> p t c", c=3)
        iota_i = accT[:, 9000:9000 + WIN].bitcast(i32)
        far_shift_i = accT[:, 9200:9200 + NB + 1].bitcast(i32)
        w2raw = accT[0:HID0 + 1, 9400:9400 + RDIM]
        rel = sb("rel", [P, NG * TPG])
        idx = sb("idx", [P, UNROLL, TPG], i32)
        rows = sb("rows", [P, UNROLL, TPG, HID])
        ew_row = sb("ew_row", [HID0, 2, GE])
        hidT = sb("hidT", [HID0 + 1, 2, TPG, P])
        onehot = sb("onehot", [P, 2, TPG, WIN])
        dist = sb("dist", [P, TPG, WIN])
        onehotX = sb("onehotX", [P, TPG, WIN])
        relX = sb("relX", [P, TPG])
        featV = sb("featV", [P, 2, TPG, 5, 16])
        featS = sb("featS", [P, 2, TPG, 16])
        dotp = sb("dotp", [P, TPG, 3, MUL])
        cross1 = sb("cross1", [P, TPG, 3, MUL])
        cross2 = sb("cross2", [P, TPG, 3, MUL])
        along = sb("along", [P, 4, 3, MUL])
        nodes = sb("nodes", [P, F + 1])
        nodesX = sb("nodesX", [P, F + 1])
        mu = sb("mu", [P, NB])
        var = sb("var", [P, NB])
        dis = sb("dis", [P, NB])
        meta_i = sb("meta_i", [NB, 2, 2], i32)
        span_i = sb("span_i", [NB, 2, 2], i32)
        meta = sb("meta", [P, NG * 2], i32)
        iota = sb("iota", [P, WIN])
        far_shift = sb("far_shift", [P, NB + 1])
        ident = sb("ident", [P, P])
        one = sb("one", [P, 1])
        flag = sb("flag", [P, 1])
        w1c = sb("w1c", [HID0, 1])
        b1c = sb("b1c", [HID0, 1])
        w2n = sb("w2n", [HID0 + 1, RDIM])
        W1s = sb("W1s", [F, HID])
        W2s = sb("W2s", [HID, HID])
        W3s = sb("W3s", [HID, F])
        B1c = sb("B1c", [HID, 1])
        B2c = sb("B2c", [HID, 1])
        B3r = sb("B3r", [P, F])

        radial = [pb(f"radial{i}", [P, 2, 512]) for i in range(2)]
        sums = pb("sums", [P, 2, 512])
        psT = pb("psT", [P, 512])
        psX = pb("psX", [P, 512])

        x_in = sem("x_in")
        x_tail = sem("x_tail")
        edges_in = sem("edges_in")
        edges_tail = sem("edges_tail")
        rows_in = sem("rows_in")
        consts_in = sem("consts_in")
        convs_in = sem("convs_in")
        root_asked = sem("root_asked")
        root_done = sem("root_done")
        made = sem("made")
        pads = sem("pads")
        prepared = sem("prepared")
        v_chain = sem("v_chain")
        meta_out = sem("meta_out")
        meta_in = sem("meta_in")
        meta_ready = sem("meta_ready")
        table_ready = [sem(f"table_ready{n}") for n in range(NLAYER)]
        table_out = [sem(f"table_out{n}") for n in range(NLAYER)]
        table_out2 = [sem(f"table_out2_{n}") for n in range(NLAYER)]
        idx_in = [sem(f"idx_in{u}") for u in range(UNROLL)]
        gathered = [sem(f"gathered{u}") for u in range(UNROLL)]
        ew_in = [sem(f"ew_in{u}") for u in range(2)]
        hid_ready = sem("hid_ready")
        rows_copied = sem("rows_copied")
        dist_ready = sem("dist_ready")
        onehot_ready = sem("onehot_ready")
        radial_ready = sem("radial_ready")
        prods_done = sem("prods_done")
        dot_ready = sem("dot_ready")
        cross_ready = sem("cross_ready")
        feats_ready = sem("feats_ready")
        scalars_ready = sem("scalars_ready")
        along_ready = sem("along_ready")
        msg_ready = sem("msg_ready")
        half_summed = sem("half_summed")
        nodes_ready = sem("nodes_ready")
        nodes_turned = sem("nodes_turned")
        added = sem("added")
        group_summed = sem("group_summed")
        far_rel = [sem(f"far_rel{n}") for n in range(NLAYER)]
        far_onehot = [sem(f"far_onehot{n}") for n in range(NLAYER)]
        far_summed = [sem(f"far_summed{n}") for n in range(NLAYER)]
        far_nodes = sem("far_nodes")
        far_turned = sem("far_turned")
        far_added = [sem(f"far_added{n}") for n in range(NLAYER)]
        blocks_turned = sem("blocks_turned")
        blocks_read = sem("blocks_read")
        feat_turned = sem("feat_turned")
        acc_set = sem("acc_set")
        norm_spread = sem("norm_spread")
        norm_set = sem("norm_set")
        mm_done = [sem(f"mm_done{n}") for n in range(2)]
        scaled = [sem(f"scaled{n}") for n in range(2)]
        relued = [sem(f"relued{n}") for n in range(2)]
        projected = sem("projected")
        next_set = [sem(f"next_set{n}") for n in range(2)]
        next_turned = [sem(f"next_turned{n}") for n in range(2)]
        next_copied = [sem(f"next_copied{n}") for n in range(2)]
        out_turned = sem("out_turned")
        out_ready = sem("out_ready")
        out_done = sem("out_done")

        block = ctx.enter_context(nc.Block())

        def sweep(eng, body):
            body(0, True, False)
            with eng.Fori(1, NIT - 1) as it:
                body(it, False, False)
            body(NIT - 1, False, True)

        CH = 4
        NCH = -(-NB // CH)
        chunks = [(c, c * CH * P, min(CH * P, NPAD - c * CH * P)) for c in range(NCH)]
        TB = 14
        NTB = NB // TB

        @block.sync
        def _(sp):
            sp.dma_start(xn[:, 0:NB - 1, :],
                         x[0:(NB - 1) * P, :].rearrange("(b p) f -> p b f", p=P)).then_inc(x_in, 16)
            sp.dma_start(dst_rows[:, 0, :], dst[0:NB * GE].rearrange("(g e) -> g e", e=GE)).then_inc(rows_in, 16)
            sp.dma_start(dst_rows[0:NB - 1, 1, :],
                         dst[NB * GE:(NG - 1) * GE].rearrange("(g e) -> g e", e=GE)).then_inc(rows_in, 16)
            sp.dma_start(dst_rows[NB - 1:NB, 1, :],
                         dst[E - GE:E].rearrange("(g e) -> g e", e=GE)).then_inc(rows_in, 16)
            sp.wait_ge(pads, 1)
            sp.dma_start(xn[0:NTAIL, NB - 1, :], x[(NB - 1) * P:N, :]).then_inc(x_tail, 16)
            full = (NG - 1) * TPG
            sp.dma_start(dst_i[:, 0:full].rearrange("p (g j) -> p g j", j=TPG),
                         dst[0:(NG - 1) * GE].rearrange("(g p j) -> p g j", p=P, j=TPG)).then_inc(edges_in, 16)
            sp.dma_start(attr[:, 0:full, :].rearrange("p (g j) c -> p g (j c)", j=TPG),
                         edge_attr[0:(NG - 1) * GE, :].rearrange("(g p j) c -> p g (j c)", p=P, j=TPG)).then_inc(edges_in, 16)
            sp.wait_ge(pads, 3)
            sp.dma_start(dst_i[0:PTAIL, full:full + TPG],
                         dst[(NG - 1) * GE:E].rearrange("(p j) -> p j", j=TPG)).then_inc(edges_tail, 16)
            sp.dma_start(attr[0:PTAIL, full:full + TPG, :].rearrange("p j c -> p (j c)"),
                         edge_attr[(NG - 1) * GE:E, :].rearrange("(p j) c -> p (j c)", j=TPG)).then_inc(edges_tail, 16)
            sp.wait_ge(meta_ready, 2)
            sp.dma_start(meta_d.rearrange("(h r) c -> r h c", r=NB), meta_i[:, :, :]).then_inc(meta_out, 16)
            sp.wait_ge(meta_out, 16)
            sp.dma_start(meta[:, :], meta_d.rearrange("g c -> (g c)").partition_broadcast(P)).then_inc(meta_in, 16)

            def load_idx(n, it, u, first, last):
                if n > 0 or not first:
                    sp.wait_ge(gathered[u], (it + n * NIT) * (16 * TPG))
                if last and u == UNROLL - 1:
                    d = idx[0:PTAIL, u, :]
                    s = src[(NG - 1) * GE:E].rearrange("(p j) -> p j", j=TPG)
                else:
                    d = idx[:, u, :]
                    s = src[bass.ds((it * UNROLL + u) * GE, GE)].rearrange("(p j) -> p j", j=TPG)
                sp.dma_start(d, s).then_inc(idx_in[u], 16)

            def load_ew(it, u, first, last):
                if not (first and u < 2):
                    sp.wait_ge(hid_ready, it * UNROLL + u - 1)
                if last and u == UNROLL - 1:
                    d = ew_row[:, u % 2, 0:ETAIL]
                    s = edge_weight[(NG - 1) * GE:E]
                else:
                    d = ew_row[:, u % 2, :]
                    s = edge_weight[bass.ds((it * UNROLL + u) * GE, GE)]
                sp.dma_start(d, s.partition_broadcast(HID0)).then_inc(ew_in[u % 2], 16)

            def layer0(it, first, last):
                for u in range(UNROLL):
                    load_idx(0, it, u, first, last)
                    load_ew(it, u, first, last)

            def table_whole(n, view):
                sp.wait_ge(table_ready[n], 1)
                sp.dma_start(tables[n].rearrange("(b p) f -> p b f", p=P), view).then_inc(table_out[n], 16)

            def table_chunks(n, width):
                for c, at, w in chunks:
                    sp.wait_ge(next_copied[n - 2], c + 1)
                    view = tbuf[:, c % 2, 0:w // P * width].rearrange("p (b f) -> p b f", f=width)
                    (sp.dma_start(tables[n][at:at + w, :].rearrange("(b p) f -> p b f", p=P), view)
                       .then_inc((table_out if c % 2 == 0 else table_out2)[n], 16))

            table_whole(0, lnA)
            sweep(sp, layer0)
            table_whole(1, lnA)
            sweep(sp, lambda it, first, last: [load_idx(1, it, u, first, last) for u in range(UNROLL)])
            table_chunks(2, HID)
            sweep(sp, lambda it, first, last: [load_idx(2, it, u, first, last) for u in range(UNROLL)])
            table_chunks(3, F)
            sweep(sp, lambda it, first, last: [load_idx(3, it, u, first, last) for u in range(UNROLL)])
            for k in range(NTB):
                sp.wait_ge(out_ready, k + 1)
                b0, b1_ = k * TB, (k + 1) * TB - (k == NTB - 1)
                sp.dma_start(out[b0 * P:b1_ * P, :].rearrange("(b p) f -> p b f", p=P),
                             lnA[:, b0:b1_, :]).then_inc(out_done, 16)
            sp.dma_start(out[(NB - 1) * P:N, :], lnA[0:NTAIL, NB - 1, :]).then_inc(out_done, 16)
            sp.wait_ge(out_done, 16 * (NTB + 1))

        @block.gpsimd
        def _(pool):
            nc.gpsimd.memset(xn[:, NB - 1, :], 0.0).then_inc(pads, 1)
            nc.gpsimd.memset(dst_i[:, (NG - 1) * TPG:NG * TPG], -WIN).then_inc(pads, 1)
            nc.gpsimd.memset(attr[:, (NG - 1) * TPG:NG * TPG, :], 1.0).then_inc(pads, 1)
            nc.gpsimd.iota(iota_i[:, :], pattern=[[1, WIN]], base=0, channel_multiplier=0).then_inc(made, 1)
            nc.gpsimd.iota(far_shift_i[:, :], pattern=[[WIN, NB + 1]], base=0, channel_multiplier=0).then_inc(made, 1)
            nc.gpsimd.memset(ident[:, :], 0.0).then_inc(made, 1)
            nc.gpsimd.memset(one[:, :], 1.0).then_inc(made, 1)
            nc.gpsimd.memset(ew_row[:, :, :], 0.0).then_inc(made, 1)
            nc.gpsimd.memset(idx[:, :, :], 0).then_inc(made, 1)
            pool.wait_ge(made, 3)
            nc.gpsimd.affine_select(out=ident[:, :], in_=ident[:, :], compare_op=ALU.not_equal, fill=1.0,
                                    base=0, pattern=[[-1, P]], channel_multiplier=1).then_inc(made, 1)

            turn = pool.alloc_register("turn_pool")

            def gathers(n):
                def body(it, first, last):
                    for u in range(UNROLL):
                        pool.wait_ge(idx_in[u], (it + n * NIT + 1) * 16)
                        free = rows_copied if n == 0 else added
                        if last:
                            pool.wait_ge(free, n * NG + it * UNROLL + u - UNROLL + 1)
                        elif not first:
                            pool.wait_ge(free, pool.snap(turn) + (n * NG + 1))
                            pool.reg_add(turn, turn, 1)
                        for j in range(TPG):
                            (pool.indirect_dma_start(rows[:, u, j, 0:WIDTH[n]], None, tables[n],
                                                     bass.IndirectOffsetOnAxis(ap=idx[:, u, j:j + 1], axis=0))
                                 .then_inc(gathered[u], 16))
                if n < 2:
                    pool.wait_ge(table_out[n], 16)
                else:
                    pool.wait_ge(table_out[n], 16 * ((NCH + 1) // 2))
                    pool.wait_ge(table_out2[n], 16 * (NCH // 2))
                pool.reg_mov(turn, 0)
                sweep(pool, body)

            for n in range(NLAYER):
                gathers(n)

        @block.scalar
        def _(act):
            act.dma_start(w1c[:, :], w1.rearrange("a n -> n a")).then_inc(consts_in, 16)
            act.dma_start(b1c[:, :], b1.rearrange("(n a) -> n a", a=1)).then_inc(consts_in, 16)
            act.dma_start(w2raw[0:HID0, :], w2).then_inc(consts_in, 16)
            act.dma_start(w2raw[HID0:HID0 + 1, :], b2.rearrange("(a n) -> a n", a=1)).then_inc(consts_in, 16)
            act.dma_start(W1s[:, :], W1).then_inc(convs_in, 16)
            act.dma_start(W2s[:, :], W2).then_inc(convs_in, 16)
            act.dma_start(W3s[:, :], W3).then_inc(convs_in, 16)
            act.dma_start(B1c[:, :], B1.rearrange("(n a) -> n a", a=1)).then_inc(convs_in, 16)
            act.dma_start(B2c[:, :], B2.rearrange("(n a) -> n a", a=1)).then_inc(convs_in, 16)
            act.dma_start(B3r[:, :], B3.partition_broadcast(P)).then_inc(convs_in, 16)

            def root(n, ap):
                act.wait_ge(root_asked, n)
                nc.scalar.activation(ap, ap, ACT.Sqrt).then_inc(root_done, 1)

            def make_onehot(n, it, u, first):
                g = it * UNROLL + u
                if n == 0:
                    if not (first and u < 2):
                        act.wait_ge(half_summed, 2 * g - 2)
                elif first and u < 2:
                    if n == 1:
                        act.wait_ge(half_summed, 2 * NG)
                    else:
                        act.wait_ge(group_summed, (n - 1) * NG)
                else:
                    act.wait_ge(group_summed, g + ((n - 1) * NG - 1))
                if n > 0 or not (first and u == 0):
                    act.wait_ge(onehot_ready, g + n * NG)
                for j in range(TPG):
                    ins = nc.scalar.activation(dist[:, j, :], iota[:, :], ACT.Abs, scale=-1.0,
                                               bias=rel[:, bass.ds(g * TPG + j, 1)])
                ins.then_inc(dist_ready, 1)
                act.wait_ge(dist_ready, g + (n * NG + 1))
                nc.scalar.activation(onehot[:, u % 2, :, :], dist[:, :, :], ACT.Relu, scale=-1.0,
                                     bias=one[:, :]).then_inc(onehot_ready, 1)

            def layer0(it, first, last):
                for u in range(UNROLL):
                    g = it * UNROLL + u
                    act.wait_ge(ew_in[u % 2], (it * 2 + u // 2 + 1) * 16)
                    if not (first and u < 2):
                        act.wait_ge(radial_ready, 4 * g - 4)
                    nc.scalar.activation(hidT[0:HID0, u % 2, :, :],
                                         ew_row[:, u % 2, :].rearrange("c (p j) -> c j p", j=TPG),
                                         ACT.Relu, bias=b1c[:, :], scale=w1c[:, :]).then_inc(hid_ready, 1)
                    make_onehot(0, it, u, first)
                    act.wait_ge(gathered[u], (it + 1) * (16 * TPG))
                    if not (first and u < 2):
                        act.wait_ge(prods_done, 4 * g - 4)
                    vec = rows[:, u, :, MUL:F].rearrange("p t (v i) -> p t i v", i=3)
                    nc.scalar.copy(featV[:, u % 2, :, 0:3, 0:MUL], vec)
                    nc.scalar.copy(featV[:, u % 2, :, 3:5, 0:MUL], vec[:, :, 0:2, :])
                    nc.scalar.copy(featS[:, u % 2, :, 0:MUL], rows[:, u, :, 0:MUL]).then_inc(rows_copied, 1)

            root(1, var[:, :])
            root(2, length[:, :])
            act.wait_ge(consts_in, 64)
            act.wait_ge(made, 7)
            act.wait_ge(prepared, 1)
            sweep(act, layer0)
            root(3, dis[:, :])
            root(4, var[:, :])
            for c, at, w in chunks:
                act.wait_ge(feat_turned, c + 1)
                nc.scalar.copy(accT[0:F, at:at + w], radial[1][0:F, c % 2, 0:w]).then_inc(acc_set, 1)
            for c, at, w in chunks:
                act.wait_ge(norm_spread, c + 1)
                nc.scalar.copy(norm_row[:, at:at + w], radial[0][:, c % 2, 0:w]).then_inc(norm_set, 1)

            def conv(n):
                sweep(act, lambda it, first, last: [make_onehot(n, it, u, first) for u in range(UNROLL)])

            def post(k):
                width = HID if k == 0 else F

                def relu(c, at, w):
                    act.wait_ge(scaled[k], c + 1)
                    if c >= 2:
                        act.wait_ge(next_set[0] if k == 0 else projected, c - 1)
                    nc.scalar.activation(rbuf[:, c % 2, 0:w], ybuf[:, c % 2, 0:w], ACT.Relu,
                                         bias=(B1c if k == 0 else B2c)[:, :]).then_inc(relued[k], 1)

                relu(*chunks[0])
                for c, at, w in chunks:
                    if c + 1 < NCH:
                        relu(*chunks[c + 1])
                    act.wait_ge(next_turned[k], c + 1)
                    if c >= 2:
                        act.wait_ge((table_out if c % 2 == 0 else table_out2)[k + 2], 16 * (c // 2))
                    used = w // P * width
                    nc.scalar.copy(tbuf[:, c % 2, 0:used], radial[1][:, c % 2, 0:used]).then_inc(next_copied[k], 1)

            conv(1)
            act.wait_ge(convs_in, 96)
            post(0)
            conv(2)
            post(1)
            conv(3)

        @block.vector
        def _(dve):
            v = nc.vector
            chain = [0]

            def link(ins):
                chain[0] += 1
                ins.then_inc(v_chain, 1)
                dve.wait_ge(v_chain, chain[0])

            roots = [0]

            def reciprocal_root(ap):
                roots[0] += 1
                v.memset(flag[:, :], 0.0).then_inc(root_asked, 1)
                dve.wait_ge(root_done, roots[0])
                link(v.reciprocal(ap, ap))

            def layernorm(src_ap, dst_ap, tmp_ap):
                link(v.tensor_reduce(mu[:, :], src_ap, X, ALU.add))
                link(v.tensor_scalar(mu[:, :], mu[:, :], 1.0 / F, None, ALU.mult))
                link(v.tensor_tensor(dst_ap, src_ap, mu[:, :].unsqueeze(2).to_broadcast([P, NB, F]), ALU.subtract))
                link(v.tensor_tensor(tmp_ap, dst_ap, dst_ap, ALU.mult))
                link(v.tensor_reduce(var[:, :], tmp_ap, X, ALU.add))
                link(v.tensor_scalar(var[:, :], var[:, :], 1.0 / F, EPS, ALU.mult, ALU.add))
                reciprocal_root(var[:, :])
                link(v.scalar_tensor_tensor(dst_ap, dst_ap, 0.0, var[:, :].unsqueeze(2).to_broadcast([P, NB, F]),
                                            ALU.max, ALU.mult))

            dve.wait_ge(x_in, 16)
            dve.wait_ge(x_tail, 16)
            layernorm(xn[:, :, :], lnA, lnB)
            link(v.memset(nodes[:, :], 0.0))
            v.memset(nodesX[:, :], 0.0).then_inc(table_ready[0], 1)

            dve.wait_ge(rows_in, 48)
            link(v.tensor_reduce(span_i[:, :, 0], dst_rows, X, ALU.min))
            link(v.tensor_reduce(span_i[:, :, 1], dst_rows, X, ALU.max))
            link(v.tensor_copy(meta_i[:, :, 0], span_i[:, :, 0]))
            link(v.tensor_tensor(span_i[:, :, 1], span_i[:, :, 1], span_i[:, :, 0], ALU.subtract))
            v.tensor_scalar(meta_i[:, :, 1], span_i[:, :, 1], WIN.bit_length() - 1, None,
                            ALU.arith_shift_right).then_inc(meta_ready, 1)
            dve.wait_ge(made, 7)
            v.tensor_copy(iota[:, :], iota_i[:, :]).then_inc(meta_ready, 1)
            link(v.tensor_copy(far_shift[:, :], far_shift_i[:, :]))
            dve.wait_ge(meta_ready, 2)
            dve.wait_ge(consts_in, 64)
            wA = w2n[:, 0:256].rearrange("k (m u g v) -> k m u g v", m=2, u=MUL, g=2)
            wB = w2n[:, 256:384].rearrange("k (u m v) -> k u m v", u=MUL, m=2)
            raw = [w2raw[:, n * 64:(n + 1) * 64].rearrange("k (u v) -> k u v", v=MUL) for n in range(3)]
            raw11 = w2raw[:, 192:384].rearrange("k (u v m) -> k u v m", u=MUL, v=MUL)
            link(v.tensor_scalar(wA[:, 1, :, 0, :], raw[0], K00, None, ALU.mult))
            link(v.tensor_scalar(wA[:, 1, :, 1, :], raw[1], K01, None, ALU.mult))
            link(v.tensor_scalar(wA[:, 0, :, 0, :], raw[2], K10, None, ALU.mult))
            link(v.tensor_scalar(wA[:, 0, :, 1, :], raw11[:, :, :, 2], K11_2, None, ALU.mult))
            link(v.tensor_scalar(wB[:, :, 1, :], raw11[:, :, :, 1], K11_1, None, ALU.mult))
            link(v.tensor_scalar(w2raw[:, 0:64], w2raw[:, 192:384].rearrange("k (n m) -> k n m", m=3)[:, :, 2],
                                 -K11_2 / 3, None, ALU.mult))
            link(v.tensor_scalar(w2raw[:, 64:128], w2raw[:, 192:384].rearrange("k (n m) -> k n m", m=3)[:, :, 0],
                                 K11_0, None, ALU.mult))
            link(v.tensor_tensor(wB[:, :, 0, :], raw[0], raw[1], ALU.add))
            dve.wait_ge(edges_in, 32)
            dve.wait_ge(edges_tail, 32)
            dve.wait_ge(meta_in, 16)
            start_all = meta[:, :].rearrange("p (g c) -> p g c", c=2)[:, :, 0:1].to_broadcast([P, NG, TPG])
            link(v.tensor_tensor(rel[:, :].rearrange("p (g j) -> p g j", j=TPG),
                                 dst_i.rearrange("p (g j) -> p g j", j=TPG), start_all, ALU.subtract))
            dve.wait_ge(table_out[0], 16)
            link(v.tensor_tensor(squares, attr, attr, ALU.mult))
            link(v.tensor_reduce(length[:, :], squares, X, ALU.add))
            reciprocal_root(length[:, :])
            inv = length[:, :].unsqueeze(2)
            link(v.tensor_tensor(direction[:, :, 0:2], attr[:, :, 1:3], inv.to_broadcast([P, NG * TPG, 2]), ALU.mult))
            link(v.tensor_tensor(direction[:, :, 2:5], attr, inv.to_broadcast([P, NG * TPG, 3]), ALU.mult))
            link(v.memset(hidT[HID0:HID0 + 1, :, :, :], 1.0))
            link(v.memset(accT[:, :], 0.0))
            link(v.memset(msg[:, :, :, 16:17], 1.0))
            v.memset(relX[:, :], 0.0).then_inc(prepared, 1)

            far_count = dve.alloc_register("far_count")

            def further(g):
                return dve.value_load(meta[0:1, bass.ds(g * 2 + 1, 1)], min_val=0, max_val=NB)

            def start_of(g):
                return dve.value_load(meta[0:1, bass.ds(g * 2, 1)], min_val=0, max_val=N - 1)

            def far_windows(n, g):
                n_far, start = further(g), start_of(g)
                with dve.If(n_far > 0):
                    with dve.Fori(1, n_far + 1) as k:
                        dve.reg_add(far_count, far_count, 1)
                        count = dve.snap(far_count)
                        v.tensor_scalar(relX[:, :], rel[:, bass.ds(g * TPG, TPG)], far_shift[:, bass.ds(k, 1)],
                                        None, ALU.subtract).then_inc(far_rel[n], 1)
                        dve.wait_ge(far_rel[n], count)
                        v.tensor_tensor(onehotX[:, :, :], iota[:, :].unsqueeze(1).to_broadcast([P, TPG, WIN]),
                                        relX[:, :].unsqueeze(2).to_broadcast([P, TPG, WIN]),
                                        ALU.is_equal).then_inc(far_onehot[n], 1)
                        dve.wait_ge(far_summed[n], count)
                        first_node = nc.s_assert_within(
                            start + k * WIN, 0, N - 1, skip_runtime_bounds_check_because=
                            "a window starts at or below its group's greatest destination")
                        at = bass.ds(first_node, WIN)
                        if n == 0:
                            v.tensor_copy(nodesX[:, 0:MUL + 1], psX[:, 0:MUL + 1])
                            v.tensor_reduce(nodesX[:, MUL + 1:F + 1],
                                            psX[:, MUL + 1:SEGW].rearrange("p (c s) -> p c s", s=16),
                                            X, ALU.add).then_inc(far_nodes, 1)
                            dve.wait_ge(far_turned, count)
                            v.tensor_tensor(accT[0:F + 1, at], accT[0:F + 1, at], psT[0:F + 1, 0:WIN],
                                            ALU.add).then_inc(far_added[n], 1)
                        else:
                            w = WIDTH[n]
                            v.tensor_tensor(accT[0:w, at], accT[0:w, at], psX[0:w, 0:WIN],
                                            ALU.add).then_inc(far_added[n], 1)
                        dve.wait_ge(far_added[n], count)

            def features(it, u):
                g, s = it * UNROLL + u, u % 2
                d = direction[:, bass.ds(g * TPG, TPG), :]
                dve.wait_ge(rows_copied, g + 1)
                shape = [P, TPG, 3, MUL]
                v.tensor_tensor(dotp[:, :, :, :], featV[:, s, :, 0:3, 0:MUL],
                                d[:, :, 0:3].unsqueeze(3).to_broadcast(shape), ALU.mult).then_inc(dot_ready, 1)
                v.tensor_tensor(cross1[:, :, :, :], featV[:, s, :, 2:5, 0:MUL],
                                d[:, :, 1:4].unsqueeze(3).to_broadcast(shape), ALU.mult)
                v.tensor_tensor(cross2[:, :, :, :], featV[:, s, :, 1:4, 0:MUL],
                                d[:, :, 2:5].unsqueeze(3).to_broadcast(shape), ALU.mult).then_inc(cross_ready, 1)
                dve.wait_ge(dot_ready, g + 1)
                v.tensor_reduce(featS[:, s, :, MUL:2 * MUL],
                                dotp[:, :, :, :].rearrange("p t i v -> p t v i"), X, ALU.add)
                dve.wait_ge(cross_ready, g + 1)
                v.tensor_tensor(featV[:, s, :, 0:3, MUL:2 * MUL], cross1[:, :, :, :], cross2[:, :, :, :],
                                ALU.subtract).then_inc(feats_ready, 1)

            def half(it, u, h, first):
                g, s = it * UNROLL + u, u % 2
                if not (first and u == 0):
                    dve.wait_ge(half_summed, 2 * g + (h - 1))
                for q in range(2):
                    dve.wait_ge(radial_ready, 4 * g + (2 * h + q + 1))
                    if h == 0 and q == 0:
                        dve.wait_ge(feats_ready, g + 1)
                    R = radial[q]
                    t = 2 * q
                    v.tensor_tensor(prodA[:, h, t:t + 2, :].rearrange("p t (m s) -> p t m s", s=16),
                                    R[:, :, 0:256].rearrange("p t (m s) -> p t m s", s=16),
                                    featS[:, s, 4 * h + t:4 * h + t + 2, :].unsqueeze(2).to_broadcast([P, 2, 16, 16]),
                                    ALU.mult)
                    for k in range(2):
                        last = v.tensor_tensor(
                            msg[:, h, t + k, 17:401].rearrange("p (i u s) -> p i u s", i=3, u=MUL),
                            R[:, k, 256:384].rearrange("p (u s) -> p u s", s=16).unsqueeze(1).to_broadcast([P, 3, MUL, 16]),
                            featV[:, s, 4 * h + t + k, 0:3, :].unsqueeze(2).to_broadcast([P, 3, MUL, 16]), ALU.mult)
                    last.then_inc(prods_done, 1)
                dve.wait_ge(prods_done, 4 * g + (2 * h + 2))
                v.tensor_reduce(msg[:, h, :, 0:16], prodA[:, h, :, :].rearrange("p t (m s) -> p t m s", s=16),
                                X, ALU.add).then_inc(scalars_ready, 1)
                dve.wait_ge(scalars_ready, 2 * g + (h + 1))
                v.tensor_tensor(along[:, :, :, :], msg[:, h, :, 0:MUL].unsqueeze(2).to_broadcast([P, 4, 3, MUL]),
                                direction[:, bass.ds(g * TPG + 4 * h, 4), 0:3].unsqueeze(3).to_broadcast([P, 4, 3, MUL]),
                                ALU.mult).then_inc(along_ready, 1)
                dve.wait_ge(along_ready, 2 * g + (h + 1))
                slot = msg[:, h, :, 17:401].rearrange("p t (n s) -> p t n s", s=16)[:, :, :, 0]
                v.tensor_tensor(slot, slot, along[:, :, :, :].rearrange("p t o u -> p t (o u)"),
                                ALU.add).then_inc(msg_ready, 1)

            def window_sums(g, parity):
                dve.wait_ge(half_summed, 2 * g + 2)
                v.tensor_copy(nodes[:, 0:MUL + 1], sums[:, parity, 0:MUL + 1])
                v.tensor_reduce(nodes[:, MUL + 1:F + 1],
                                sums[:, parity, MUL + 1:SEGW].rearrange("p (c s) -> p c s", s=16),
                                X, ALU.add).then_inc(nodes_ready, 1)

            def window_add(g, start):
                dve.wait_ge(nodes_turned, g + 1)
                if not isinstance(g, int) or g > 0:
                    dve.wait_ge(added, g)
                at = bass.ds(start, WIN)
                v.tensor_tensor(accT[0:F + 1, at], accT[0:F + 1, at], psT[0:F + 1, 0:WIN],
                                ALU.add).then_inc(added, 1)

            def layer0(it, first, last):
                for u in range(UNROLL):
                    g = it * UNROLL + u
                    features(it, u)
                    half(it, u, 0, first)
                    if not (first and u == 0):
                        window_sums(g - 1, (u - 1) % 2)
                    half(it, u, 1, first)
                    if not (first and u == 0):
                        window_add(g - 1, start_of(g - 1))
                    far_windows(0, g)

            dve.reg_mov(far_count, 0)
            sweep(dve, layer0)
            window_sums(NG - 1, (NG - 1) % 2)
            window_add(NG - 1, start_of(NG - 1))

            for k in range(NTB):
                dve.wait_ge(blocks_turned, k + 1)
                bs = slice(k * TB, (k + 1) * TB)
                ps = radial[0][:, k % 2, 0:TB * (F + 1)].rearrange("p (b c) -> p b c", c=F + 1)
                v.tensor_tensor(xn[:, bs, 0:MUL], xn[:, bs, 0:MUL], ps[:, :, 0:MUL], ALU.add)
                xv = xn[:, bs, MUL:F].rearrange("p b (u o) -> p b o u", o=3)
                v.tensor_tensor(xv, xv, ps[:, :, MUL + 1:F + 1].rearrange("p b (o u) -> p b o u", o=3), ALU.add)
                v.tensor_scalar(dis[:, bs], ps[:, :, MUL], 1.0, None, ALU.add).then_inc(blocks_read, 1)
            dve.wait_ge(blocks_read, NTB)
            reciprocal_root(dis[:, :])
            layernorm(xn[:, :, :], lnA, lnB)
            v.tensor_tensor(lnA, lnA, dis[:, :].unsqueeze(2).to_broadcast([P, NB, F]),
                            ALU.mult).then_inc(table_ready[1], 1)

            def conv(n):
                w = WIDTH[n]

                def body(it, first, last):
                    for u in range(UNROLL):
                        g = it * UNROLL + u
                        far_windows(n, g)
                        start = start_of(g)
                        dve.wait_ge(group_summed, g + ((n - 1) * NG + 1))
                        dve.wait_ge(added, g + n * NG)
                        at = bass.ds(start, WIN)
                        v.tensor_tensor(accT[0:w, at], accT[0:w, at], sums[0:w, u % 2, 0:WIN],
                                        ALU.add).then_inc(added, 1)
                dve.reg_mov(far_count, 0)
                sweep(dve, body)

            def post(k):
                def scale(c, at, w):
                    dve.wait_ge(mm_done[k], c + 1)
                    if c >= 2:
                        dve.wait_ge(relued[k], c - 1)
                    v.tensor_tensor(ybuf[:, c % 2, 0:w], radial[0][:, c % 2, 0:w], norm_row[:, at:at + w],
                                    ALU.mult).then_inc(scaled[k], 1)

                scale(*chunks[0])
                for c, at, w in chunks:
                    if c + 1 < NCH:
                        scale(*chunks[c + 1])
                    if k == 0:
                        dve.wait_ge(relued[k], c + 1)
                        v.tensor_tensor(accT[:, at:at + w], rbuf[:, c % 2, 0:w], norm_row[:, at:at + w],
                                        ALU.mult).then_inc(next_set[k], 1)
                    else:
                        dve.wait_ge(projected, c + 1)
                        v.tensor_tensor(accT[0:F, at:at + w], sums[0:F, c % 2, 0:w], norm_row[0:F, at:at + w],
                                        ALU.mult).then_inc(next_set[k], 1)
                dve.wait_ge(next_set[k], NCH)

            dve.wait_ge(acc_set, NCH)
            conv(1)
            dve.wait_ge(norm_set, NCH)
            post(0)
            conv(2)
            post(1)
            conv(3)

            dve.wait_ge(convs_in, 96)
            for k in range(NTB):
                dve.wait_ge(out_turned, k + 1)
                bs = slice(k * TB, (k + 1) * TB)
                ps = radial[0][:, k % 2, 0:TB * F].rearrange("p (b c) -> p b c", c=F)
                link(v.tensor_tensor(lnA[:, bs, :], ps, dis[:, bs].unsqueeze(2).to_broadcast([P, TB, F]), ALU.mult))
                link(v.tensor_tensor(lnA[:, bs, :], lnA[:, bs, :], B3r[:, :].unsqueeze(1).to_broadcast([P, TB, F]),
                                     ALU.add))
                v.scalar_tensor_tensor(lnA[:, bs, :], lnA[:, bs, :], 0.0, xn[:, bs, :],
                                       ALU.max, ALU.add).then_inc(out_ready, 1)

        @block.tensor
        def _(pe):
            far_count = pe.alloc_register("far_count_pe")
            turn = pe.alloc_register("turn_pe")

            def far_windows(n, g):
                n_far = pe.value_load(meta[0:1, bass.ds(g * 2 + 1, 1)], min_val=0, max_val=NB)
                with pe.If(n_far > 0):
                    with pe.Fori(1, n_far + 1):
                        count = pe.snap(far_count) + 1
                        pe.wait_ge(far_onehot[n], count)
                        for j in range(TPG):
                            if n == 0:
                                last = nc.tensor.matmul(psX[:, 0:SEGW], onehotX[:, j, :],
                                                        msg[:, j // 4, j % 4, MUL:MUL + SEGW],
                                                        start=(j == 0), stop=(j == TPG - 1))
                            else:
                                last = nc.tensor.matmul(psX[0:WIDTH[n], 0:WIN], far_rows[j], onehotX[:, j, :],
                                                        start=(j == 0), stop=(j == TPG - 1))
                        last.then_inc(far_summed[n], 1)
                        if n == 0:
                            pe.wait_ge(far_nodes, count)
                            pe.reg_add(far_count, far_count, 1)
                            nc.tensor.transpose(psT[0:F + 1, 0:P], nodesX[:, :], ident[:, :]).then_inc(far_turned, 1)
                        else:
                            pe.reg_add(far_count, far_count, 1)

            def radial_pair(g, s, q, free):
                if q == 0:
                    pe.wait_ge(hid_ready, g + 1)
                if free:
                    pe.wait_ge(prods_done, 4 * g + (q - 1))
                for k in range(2):
                    last = nc.tensor.matmul(radial[q % 2][:, k, 0:RDIM], hidT[:, s, 2 * q + k, :], w2n[:, :],
                                            start=True, stop=True)
                last.then_inc(radial_ready, 1)

            def sum_half(it, u, h, first):
                g, s = it * UNROLL + u, u % 2
                pe.wait_ge(msg_ready, 2 * g + (h + 1))
                if h == 0:
                    pe.wait_ge(onehot_ready, g + 1)
                    if not (first and u < 2):
                        pe.wait_ge(nodes_ready, g - 1)
                for k in range(4):
                    last = nc.tensor.matmul(sums[:, s, 0:SEGW], onehot[:, s, 4 * h + k, :],
                                            msg[:, h, k, MUL:MUL + SEGW],
                                            start=(h == 0 and k == 0), stop=(h == 1 and k == 3))
                last.then_inc(half_summed, 1)

            def turn_nodes(g):
                in_loop = not isinstance(g, int)
                if in_loop:
                    g = pe.snap(turn) + (UNROLL - 1)
                pe.wait_ge(nodes_ready, g + 1)
                if in_loop or g > 0:
                    pe.wait_ge(added, g)
                if in_loop:
                    pe.reg_add(turn, turn, 1)
                nc.tensor.transpose(psT[0:F + 1, 0:P], nodes[:, :], ident[:, :]).then_inc(nodes_turned, 1)

            def layer0(it, first, last):
                for u in range(UNROLL):
                    g, s = it * UNROLL + u, u % 2
                    radial_pair(g, s, 2, True)
                    radial_pair(g, s, 3, True)
                    sum_half(it, u, 0, first)
                    if not (first and u == 0):
                        turn_nodes(g - 1)
                    if not (last and u == UNROLL - 1):
                        radial_pair(g + 1, 1 - s, 0, True)
                        radial_pair(g + 1, 1 - s, 1, True)
                    sum_half(it, u, 1, first)
                    far_windows(0, g)

            pe.wait_ge(made, 7)
            pe.wait_ge(prepared, 1)
            pe.wait_ge(meta_in, 16)
            pe.reg_mov(far_count, 0)
            pe.reg_mov(turn, 0)
            radial_pair(0, 0, 0, False)
            radial_pair(0, 0, 1, False)
            sweep(pe, layer0)
            turn_nodes(NG - 1)

            pe.wait_ge(added, NG)
            for k in range(NTB):
                if k >= 2:
                    pe.wait_ge(blocks_read, k - 1)
                for j in range(TB):
                    at = (k * TB + j) * P
                    last = nc.tensor.transpose(radial[0][:, k % 2, j * (F + 1):(j + 1) * (F + 1)],
                                               accT[0:F + 1, at:at + P], ident[0:F + 1, 0:F + 1])
                last.then_inc(blocks_turned, 1)
            pe.wait_ge(table_ready[1], 1)
            for c, at, w in chunks:
                if c >= 2:
                    pe.wait_ge(acc_set, c - 1)
                for j in range(w // P):
                    last = nc.tensor.transpose(radial[1][0:F, c % 2, j * P:(j + 1) * P],
                                               lnA[:, c * CH + j, :], ident[:, :])
                last.then_inc(feat_turned, 1)
            for c, at, w in chunks:
                if c >= 2:
                    pe.wait_ge(norm_set, c - 1)
                for j in range(w // P):
                    b = c * CH + j
                    last = nc.tensor.matmul(radial[0][:, c % 2, j * P:(j + 1) * P],
                                            dis[:, b:b + 1].to_broadcast([P, P]), ident[:, :],
                                            start=True, stop=True)
                last.then_inc(norm_spread, 1)

            def conv(n):
                w = WIDTH[n]

                def body(it, first, last):
                    for u in range(UNROLL):
                        g = it * UNROLL + u
                        pe.wait_ge(gathered[u], (it + n * NIT + 1) * (16 * TPG))
                        pe.wait_ge(onehot_ready, g + (n * NG + 1))
                        pe.wait_ge(added, g + (n * NG - 1))
                        for j in range(TPG):
                            mm = nc.tensor.matmul(sums[0:w, u % 2, 0:WIN], rows[:, u, j, 0:w],
                                                  onehot[:, u % 2, j, :], start=(j == 0), stop=(j == TPG - 1))
                        mm.then_inc(group_summed, 1)
                        for j in range(TPG):
                            far_rows[j] = rows[:, u, j, 0:w]
                        far_windows(n, g)
                pe.reg_mov(far_count, 0)
                sweep(pe, body)

            def post(k):
                width = HID if k == 0 else F
                rows_in_acc = F if k == 0 else HID

                def weigh(c, at, w):
                    if c >= 2:
                        pe.wait_ge(scaled[k], c - 1)
                    nc.tensor.matmul(radial[0][:, c % 2, 0:w], (W1s if k == 0 else W2s)[:, :],
                                     accT[0:rows_in_acc, at:at + w], start=True, stop=True).then_inc(mm_done[k], 1)

                pe.wait_ge(added, (k + 2) * NG)
                weigh(*chunks[0])
                for c, at, w in chunks:
                    if c + 1 < NCH:
                        weigh(*chunks[c + 1])
                    if k == 1:
                        pe.wait_ge(relued[k], c + 1)
                        if c >= 2:
                            pe.wait_ge(next_set[k], c - 1)
                        nc.tensor.matmul(sums[0:F, c % 2, 0:w], W3s[:, :], rbuf[:, c % 2, 0:w],
                                         start=True, stop=True).then_inc(projected, 1)
                    pe.wait_ge(next_set[k], c + 1)
                    if c >= 2:
                        pe.wait_ge(next_copied[k], c - 1)
                    for j in range(w // P):
                        last = nc.tensor.transpose(radial[1][:, c % 2, j * width:(j + 1) * width],
                                                   accT[0:width, at + j * P:at + (j + 1) * P],
                                                   ident[0:width, 0:width])
                    last.then_inc(next_turned[k], 1)

            far_rows = [None] * TPG
            conv(1)
            pe.wait_ge(convs_in, 96)
            post(0)
            conv(2)
            post(1)
            conv(3)
            pe.wait_ge(added, NLAYER * NG)
            for k in range(NTB):
                if k >= 2:
                    pe.wait_ge(out_ready, k - 1)
                for j in range(TB):
                    at = (k * TB + j) * P
                    last = nc.tensor.transpose(radial[0][:, k % 2, j * F:(j + 1) * F],
                                               accT[0:F, at:at + P], ident[0:F, 0:F])
                last.then_inc(out_turned, 1)


_INS = ["x", "src", "dst", "edge_attr_3", "edge_weight", "L0_gnn_w1", "L0_gnn_b1", "L0_gnn_w2", "L0_gnn_b2",
        "L1_gnn_W1", "L1_gnn_b1", "L1_gnn_W2", "L1_gnn_b2", "L1_gnn_W3", "L1_gnn_b3"]


def kernel(**inputs):
    import numpy as np
    import concourse.bacc as bacc
    from concourse.bass_utils import run_bass_kernel_spmd

    nc = bacc.Bacc("TRN2", target_bir_lowering=False, num_devices=1)
    arrays, args = {}, []
    for name in _INS:
        a = np.ascontiguousarray(inputs[name])
        arrays[f"in_{name}"] = a
        args.append(nc.dram_tensor(f"in_{name}", a.shape, mybir.dt.from_np(a.dtype), kind="ExternalInput").ap())
    args.append(nc.dram_tensor("out", (N, F), fp32, kind="ExternalOutput").ap())
    gnn_kernel(nc, *args)
    r = run_bass_kernel_spmd(nc, [arrays], core_ids=[0])
    return r.results[0]["out"]
```

```python
import concourse.bass as bass
from concourse import mybir
from contextlib import ExitStack
from math import pi, sqrt

P = 128
N = 12500
E = 200000
F = 32
MUL = 8
NB = -(-N // P)
NPAD = NB * P
NTAIL = N - (NB - 1) * P
TPG = 8
GE = TPG * P
NG = -(-E // GE)
UNROLL = 4
NIT = NG // UNROLL
ETAIL = E - (NG - 1) * GE
PTAIL = ETAIL // TPG
WIN = 128
RDIM = 6 * MUL * MUL
HID0 = 64
HID = 128
NLAYER = 4
WIDTH = [F, F, HID, F]
EPS = 1e-5
SEGW = MUL + 1 + 24 * 16
assert NG % UNROLL == 0 and PTAIL * TPG == ETAIL

NORM0 = sqrt(4 * pi) / sqrt(2 * MUL)
NORM1 = sqrt(4 * pi) * sqrt(3) / sqrt(4 * MUL)
Y0 = 0.5 / sqrt(pi)
Y1 = sqrt(3 / (4 * pi))
K00 = NORM0 * Y0
K01 = NORM0 * Y1 / sqrt(3)
K10 = NORM1 * Y1 / sqrt(3)
K11_0 = NORM1 * Y0 / sqrt(3)
K11_1 = NORM1 * Y1 / sqrt(6)
K11_2 = NORM1 * sqrt(3 / (8 * pi))

IN_RANGE = "the tables hold least destinations, in [0, N), and (greatest - least) / 128, below NB"

fp32 = mybir.dt.float32
i32 = mybir.dt.int32
ALU = mybir.AluOpType
ACT = mybir.ActivationFunctionType
X = mybir.AxisListType.X


def gnn_kernel(nc, x, src, dst, edge_attr, edge_weight, w1, b1, w2, b2,
               W1, B1, W2, B2, W3, B3, out):
    ctx = ExitStack()
    with ctx:
        def sb(name, shape, dt=fp32):
            return ctx.enter_context(nc.sbuf_tensor(name, shape, dt))

        def pb(name, shape, dt=fp32):
            return ctx.enter_context(nc.psum_tensor(name, shape, dt))

        def sem(name):
            return ctx.enter_context(nc.semaphore(name))

        tables = [nc.dram_tensor(f"table{n}", [NPAD, WIDTH[n]], fp32, kind="Internal").ap()
                  for n in range(NLAYER)]
        meta_d = nc.dram_tensor("meta_d", [NG, 2], i32, kind="Internal").ap()

        accT = sb("accT", [P, NPAD + WIN])
        arena = sb("arena", [P, NPAD])
        direction = arena[:, 0:NG * TPG * 5].rearrange("p (t c) -> p t c", c=5)
        norm_row = arena[:, :]
        xn = sb("xn", [P, NB, F])
        scratch = sb("scratch", [P, 2 * NB * F])
        msg = scratch[:, 0:2 * 4 * 401].rearrange("p (h t c) -> p h t c", h=2, t=4)
        prodA = scratch[:, 3208:3208 + 2 * 4 * 256].rearrange("p (h t c) -> p h t c", h=2, t=4)
        lnA = scratch[:, 0:NB * F].rearrange("p (b f) -> p b f", f=F)
        lnB = scratch[:, NB * F:2 * NB * F].rearrange("p (b f) -> p b f", f=F)
        ybuf = scratch[:, 0:1024].rearrange("p (s n) -> p s n", s=2)
        rbuf = scratch[:, 1024:2048].rearrange("p (s n) -> p s n", s=2)
        tbuf = scratch[:, 2048:3072].rearrange("p (s n) -> p s n", s=2)
        squares = scratch[:, 0:NG * TPG * 3].rearrange("p (t c) -> p t c", c=3)
        length = scratch[:, NG * TPG * 3:NG * TPG * 4]
        dst_rows = accT[0:NB, 0:2 * GE].bitcast(i32).rearrange("p (h e) -> p h e", h=2)
        dst_i = accT[:, 2048:2048 + NG * TPG].bitcast(i32)
        attr = accT[:, 4096:4096 + NG * TPG * 3].rearrange("p (t c) -> p t c", c=3)
        iota_i = accT[:, 9000:9000 + WIN].bitcast(i32)
        far_shift_i = accT[:, 9200:9200 + NB + 1].bitcast(i32)
        w2raw = accT[0:HID0 + 1, 9400:9400 + RDIM]
        meta = accT[:, 10000:10000 + NG * 2].bitcast(i32)
        rel = sb("rel", [P, NG * TPG])
        idx = sb("idx", [P, UNROLL, TPG], i32)
        rows = sb("rows", [P, UNROLL, TPG, HID])
        ew_row = sb("ew_row", [HID0, 2, GE])
        hidT = sb("hidT", [HID0 + 1, 2, TPG, P])
        onehot = sb("onehot", [P, 2, TPG, WIN])
        dist = sb("dist", [P, TPG, WIN])
        onehotX = sb("onehotX", [P, TPG, WIN])
        relX = sb("relX", [P, TPG])
        featV = sb("featV", [P, 2, TPG, 3, 16])
        vectors = arena[:, 8000:8000 + 2 * TPG * 5 * MUL].rearrange(
            "p (s t i v) -> p s t i v", s=2, t=TPG, i=5)
        featS = sb("featS", [P, 2, TPG, 16])
        dotp = sb("dotp", [P, TPG, 3, MUL])
        cross1 = sb("cross1", [P, TPG, 3, MUL])
        cross2 = sb("cross2", [P, TPG, 3, MUL])
        along = sb("along", [P, 4, 3, MUL])
        nodes = sb("nodes", [P, F + 1])
        nodesX = sb("nodesX", [P, F + 1])
        mu = sb("mu", [P, NB])
        var = sb("var", [P, NB])
        dis = sb("dis", [P, NB])
        meta_i = sb("meta_i", [NB, 2, 2], i32)
        span_i = sb("span_i", [NB, 2, 2], i32)
        starts = sb("starts", [1, NG + 4], i32)
        late_starts = sb("late_starts", [1, NG + 4], i32)
        further = sb("further", [1, NG + 4], i32)
        iota = sb("iota", [P, WIN])
        far_shift = sb("far_shift", [P, NB + 1])
        ident = sb("ident", [P, P])
        one = sb("one", [P, 1])
        flag = sb("flag", [P, 1])
        w1c = sb("w1c", [HID0, 1])
        b1c = sb("b1c", [HID0, 1])
        w2n = sb("w2n", [HID0 + 1, RDIM])
        W1s = sb("W1s", [F, HID])
        W2s = sb("W2s", [HID, HID])
        W3s = sb("W3s", [HID, F])
        B1c = sb("B1c", [HID, 1])
        B2c = sb("B2c", [HID, 1])
        B3r = sb("B3r", [P, F])

        radial = [pb(f"radial{i}", [P, 2, 512]) for i in range(2)]
        sums = pb("sums", [P, 2, 512])
        psT = pb("psT", [P, 512])
        psX = pb("psX", [P, 512])

        def sems(name, count=UNROLL):
            return [sem(f"{name}{i}") for i in range(count)]

        x_in = sem("x_in")
        x_tail = sem("x_tail")
        edges_in = sem("edges_in")
        edges_tail = sem("edges_tail")
        rows_in = sem("rows_in")
        consts_in = sem("consts_in")
        convs_in = sem("convs_in")
        root_asked = sem("root_asked")
        root_done = sem("root_done")
        made = sem("made")
        pads = sem("pads")
        prepared = sem("prepared")
        v_chain = sem("v_chain")
        meta_out = sem("meta_out")
        meta_in = sem("meta_in")
        meta_ready = sem("meta_ready")
        table_ready = sems("table_ready", 2)
        table_out = sems("table_out", NLAYER)
        table_odd_out = sems("table_odd_out", 2)
        idx_in = [sem(f"idx_in{u}") for u in range(UNROLL)]
        gathered = [sem(f"gathered{u}") for u in range(UNROLL)]
        ew_in = sems("ew_in")
        hid_ready = sems("hid_ready")
        rows_copied = sems("rows_copied")
        dist_ready = sems("dist_ready", 2)
        onehot_ready = sems("onehot_ready")
        radial_ready = sems("radial_ready", 8)
        prods_done = sems("prods_done", 8)
        scalar_prods = sems("scalar_prods")
        feat_along_ready = sems("feat_along_ready", 2)
        dot_ready = sems("dot_ready", 2)
        cross_ready = sems("cross_ready")
        feats_ready = sems("feats_ready")
        scalars_ready = sems("scalars_ready")
        along_ready = sems("along_ready")
        msg_ready = sems("msg_ready")
        half_summed = sems("half_summed")
        nodes_ready = sems("nodes_ready")
        nodes_turned = sems("nodes_turned")
        added = sems("added")
        group_summed = sems("group_summed")
        far_rel = [sem(f"far_rel{n}") for n in range(NLAYER)]
        far_onehot = [sem(f"far_onehot{n}") for n in range(NLAYER)]
        far_summed = [sem(f"far_summed{n}") for n in range(NLAYER)]
        far_nodes = sem("far_nodes")
        far_turned = sem("far_turned")
        far_added = [sem(f"far_added{n}") for n in range(NLAYER)]
        blocks_turned = sem("blocks_turned")
        blocks_read = sem("blocks_read")
        feat_turned = sem("feat_turned")
        acc_set = sem("acc_set")
        norm_spread = sem("norm_spread")
        norm_set = sem("norm_set")
        mm_done = [sem(f"mm_done{n}") for n in range(2)]
        scaled = [sem(f"scaled{n}") for n in range(2)]
        relued = [sem(f"relued{n}") for n in range(2)]
        projected = sem("projected")
        next_set = [sem(f"next_set{n}") for n in range(2)]
        next_turned = [sem(f"next_turned{n}") for n in range(2)]
        next_copied = [sem(f"next_copied{n}") for n in range(2)]
        out_turned = sem("out_turned")
        out_ready = sem("out_ready")
        out_done = sem("out_done")

        block = ctx.enter_context(nc.Block())

        class Step:
            def __init__(self, eng, it):
                self.eng, self.it, self.known = eng, it, {}
                self.peeled = isinstance(it, int)

            def times(self, factor, plus):
                if self.peeled:
                    return self.it * factor + plus
                if (factor, plus) not in self.known:
                    self.known[factor, plus] = self.eng.snap(
                        self.it * factor + plus, min_val=factor + plus, max_val=(NIT - 2) * factor + plus)
                return self.known[factor, plus]

            def tile(self, u):
                return self.times(UNROLL * TPG, u * TPG)

        def when(sems, step, event, each=1, layer=0):
            n = len(sems)
            rounds = UNROLL * each // n
            return sems[event % n], step.times(rounds, layer * NIT * rounds + event // n + 1)

        def sweep(eng, body):
            body(Step(eng, 0), True, False)
            with eng.Fori(1, NIT - 1) as it:
                body(Step(eng, it), False, False)
            body(Step(eng, NIT - 1), False, True)

        first_step = Step(None, 0)
        last_step = Step(None, NIT - 1)

        CH = 4
        NCH = -(-NB // CH)
        chunks = [(c, c * CH * P, min(CH * P, NPAD - c * CH * P)) for c in range(NCH)]
        TB = 14
        NTB = NB // TB

        @block.sync
        def _(sp):
            sp.dma_start(xn[:, 0:NB - 1, :],
                         x[0:(NB - 1) * P, :].rearrange("(b p) f -> p b f", p=P)).then_inc(x_in, 16)
            sp.dma_start(dst_rows[:, 0, :], dst[0:NB * GE].rearrange("(g e) -> g e", e=GE)).then_inc(rows_in, 16)
            sp.dma_start(dst_rows[0:NB - 1, 1, :],
                         dst[NB * GE:(NG - 1) * GE].rearrange("(g e) -> g e", e=GE)).then_inc(rows_in, 16)
            sp.dma_start(dst_rows[NB - 1:NB, 1, :],
                         dst[E - GE:E].rearrange("(g e) -> g e", e=GE)).then_inc(rows_in, 16)
            sp.wait_ge(pads, 1)
            sp.dma_start(xn[0:NTAIL, NB - 1, :], x[(NB - 1) * P:N, :]).then_inc(x_tail, 16)
            full = (NG - 1) * TPG
            sp.dma_start(dst_i[:, 0:full].rearrange("p (g j) -> p g j", j=TPG),
                         dst[0:(NG - 1) * GE].rearrange("(g p j) -> p g j", p=P, j=TPG)).then_inc(edges_in, 16)
            sp.dma_start(attr[:, 0:full, :].rearrange("p (g j) c -> p g (j c)", j=TPG),
                         edge_attr[0:(NG - 1) * GE, :].rearrange("(g p j) c -> p g (j c)", p=P, j=TPG)).then_inc(edges_in, 16)
            sp.wait_ge(pads, 3)
            sp.dma_start(dst_i[0:PTAIL, full:full + TPG],
                         dst[(NG - 1) * GE:E].rearrange("(p j) -> p j", j=TPG)).then_inc(edges_tail, 16)
            sp.dma_start(attr[0:PTAIL, full:full + TPG, :].rearrange("p j c -> p (j c)"),
                         edge_attr[(NG - 1) * GE:E, :].rearrange("(p j) c -> p (j c)", j=TPG)).then_inc(edges_tail, 16)
            sp.wait_ge(meta_ready, 2)
            sp.dma_start(meta_d.rearrange("(h r) c -> r h c", r=NB), meta_i[:, :, :]).then_inc(meta_out, 16)
            sp.wait_ge(meta_out, 16)
            sp.dma_start(meta[:, :], meta_d.rearrange("g c -> (g c)").partition_broadcast(P)).then_inc(meta_in, 16)

            def load_idx(n, step, u, first, last):
                if n > 0 or not first:
                    sp.wait_ge(gathered[u], step.times(16 * TPG, n * NIT * 16 * TPG))
                if last and u == UNROLL - 1:
                    d = idx[0:PTAIL, u, :]
                    s = src[(NG - 1) * GE:E].rearrange("(p j) -> p j", j=TPG)
                else:
                    d = idx[:, u, :]
                    s = src[bass.ds(step.times(UNROLL * GE, u * GE), GE)].rearrange("(p j) -> p j", j=TPG)
                sp.dma_start(d, s).then_inc(idx_in[u], 16)

            def load_ew(step, u, first, last):
                if not (first and u < 2):
                    sp.wait_ge(*when(hid_ready, step, u - 2))
                if last and u == UNROLL - 1:
                    d = ew_row[:, u % 2, 0:ETAIL]
                    s = edge_weight[(NG - 1) * GE:E]
                else:
                    d = ew_row[:, u % 2, :]
                    s = edge_weight[bass.ds(step.times(UNROLL * GE, u * GE), GE)]
                sp.dma_start(d, s.partition_broadcast(HID0)).then_inc(ew_in[u], 16)

            def layer0(step, first, last):
                for u in range(UNROLL):
                    load_idx(0, step, u, first, last)
                    load_ew(step, u, first, last)

            def table_whole(n, view):
                sp.wait_ge(table_ready[n], 1)
                sp.dma_start(tables[n].rearrange("(b p) f -> p b f", p=P), view).then_inc(table_out[n], 16)

            def table_chunks(n, width):
                for c, at, w in chunks:
                    sp.wait_ge(next_copied[n - 2], c + 1)
                    view = tbuf[:, c % 2, 0:w // P * width].rearrange("p (b f) -> p b f", f=width)
                    (sp.dma_start(tables[n][at:at + w, :].rearrange("(b p) f -> p b f", p=P), view)
                       .then_inc(table_out[n] if c % 2 == 0 else table_odd_out[n - 2], 16))

            table_whole(0, lnA)
            sweep(sp, layer0)
            table_whole(1, lnA)
            sweep(sp, lambda step, first, last: [load_idx(1, step, u, first, last) for u in range(UNROLL)])
            table_chunks(2, HID)
            sweep(sp, lambda step, first, last: [load_idx(2, step, u, first, last) for u in range(UNROLL)])
            table_chunks(3, F)
            sweep(sp, lambda step, first, last: [load_idx(3, step, u, first, last) for u in range(UNROLL)])
            for k in range(NTB):
                sp.wait_ge(out_ready, k + 1)
                b0, b1_ = k * TB, (k + 1) * TB - (k == NTB - 1)
                sp.dma_start(out[b0 * P:b1_ * P, :].rearrange("(b p) f -> p b f", p=P),
                             lnA[:, b0:b1_, :]).then_inc(out_done, 16)
            sp.dma_start(out[(NB - 1) * P:N, :], lnA[0:NTAIL, NB - 1, :]).then_inc(out_done, 16)
            sp.wait_ge(out_done, 16 * (NTB + 1))

        @block.gpsimd
        def _(pool):
            nc.gpsimd.memset(xn[:, NB - 1, :], 0.0).then_inc(pads, 1)
            nc.gpsimd.memset(dst_i[:, (NG - 1) * TPG:NG * TPG], -WIN).then_inc(pads, 1)
            nc.gpsimd.memset(attr[:, (NG - 1) * TPG:NG * TPG, :], 1.0).then_inc(pads, 1)
            nc.gpsimd.iota(iota_i[:, :], pattern=[[1, WIN]], base=0, channel_multiplier=0).then_inc(made, 1)
            nc.gpsimd.iota(far_shift_i[:, :], pattern=[[WIN, NB + 1]], base=0, channel_multiplier=0).then_inc(made, 1)
            nc.gpsimd.memset(ident[:, :], 0.0).then_inc(made, 1)
            nc.gpsimd.memset(one[:, :], 1.0).then_inc(made, 1)
            nc.gpsimd.memset(ew_row[:, :, :], 0.0).then_inc(made, 1)
            nc.gpsimd.memset(idx[:, :, :], 0).then_inc(made, 1)
            pool.wait_ge(made, 3)
            nc.gpsimd.affine_select(out=ident[:, :], in_=ident[:, :], compare_op=ALU.not_equal, fill=1.0,
                                    base=0, pattern=[[-1, P]], channel_multiplier=1).then_inc(made, 1)

            turn = [pool.alloc_register(f"turn_pool{u}") for u in range(UNROLL)]

            def gathers(n):
                def body(step, first, last):
                    for u in range(UNROLL):
                        pool.wait_ge(idx_in[u], step.times(16, 16 * (n * NIT + 1)))
                        free = (rows_copied if n == 0 else added)[u]
                        if last:
                            pool.wait_ge(free, NIT - 1 + n * NIT)
                        elif not first:
                            pool.wait_ge(free, pool.snap(turn[u]) + (n * NIT + 1))
                            pool.reg_add(turn[u], turn[u], 1)
                        for j in range(TPG):
                            (pool.indirect_dma_start(rows[:, u, j, 0:WIDTH[n]], None, tables[n],
                                                     bass.IndirectOffsetOnAxis(ap=idx[:, u, j:j + 1], axis=0))
                                 .then_inc(gathered[u], 16))
                if n < 2:
                    pool.wait_ge(table_out[n], 16)
                else:
                    pool.wait_ge(table_out[n], 16 * ((NCH + 1) // 2))
                    pool.wait_ge(table_odd_out[n - 2], 16 * (NCH // 2))
                for u in range(UNROLL):
                    pool.reg_mov(turn[u], 0)
                sweep(pool, body)

            for n in range(NLAYER):
                gathers(n)

        @block.scalar
        def _(act):
            act.dma_start(w1c[:, :], w1.rearrange("a n -> n a")).then_inc(consts_in, 16)
            act.dma_start(b1c[:, :], b1.rearrange("(n a) -> n a", a=1)).then_inc(consts_in, 16)
            act.dma_start(w2raw[0:HID0, :], w2).then_inc(consts_in, 16)
            act.dma_start(w2raw[HID0:HID0 + 1, :], b2.rearrange("(a n) -> a n", a=1)).then_inc(consts_in, 16)
            act.dma_start(W1s[:, :], W1).then_inc(convs_in, 16)
            act.dma_start(W2s[:, :], W2).then_inc(convs_in, 16)
            act.dma_start(W3s[:, :], W3).then_inc(convs_in, 16)
            act.dma_start(B1c[:, :], B1.rearrange("(n a) -> n a", a=1)).then_inc(convs_in, 16)
            act.dma_start(B2c[:, :], B2.rearrange("(n a) -> n a", a=1)).then_inc(convs_in, 16)
            act.dma_start(B3r[:, :], B3.partition_broadcast(P)).then_inc(convs_in, 16)

            def root(n, ap):
                act.wait_ge(root_asked, n)
                nc.scalar.activation(ap, ap, ACT.Sqrt).then_inc(root_done, 1)

            def make_onehot(n, step, u, first):
                if n == 0:
                    if not (first and u < 2):
                        act.wait_ge(*when(half_summed, step, 2 * (u - 2) + 1, each=2))
                elif n == 1 and first and u < 2:
                    act.wait_ge(*when(half_summed, step, 2 * (u - 2) + 1, each=2, layer=1))
                else:
                    act.wait_ge(*when(group_summed, step, u - 2, layer=n - 1))
                if n > 0 or not (first and u == 0):
                    act.wait_ge(*when(onehot_ready, step, u - 1, layer=n))
                for j in range(TPG):
                    ins = nc.scalar.activation(dist[:, j, :], iota[:, :], ACT.Abs, scale=-1.0,
                                               bias=rel[:, bass.ds(step.tile(u) + j, 1)])
                ins.then_inc(dist_ready[u % 2], 1)
                act.wait_ge(*when(dist_ready, step, u, layer=n))
                nc.scalar.activation(onehot[:, u % 2, :, :], dist[:, :, :], ACT.Relu, scale=-1.0,
                                     bias=one[:, :]).then_inc(onehot_ready[u], 1)

            def layer0(step, first, last):
                for u in range(UNROLL):
                    act.wait_ge(ew_in[u], step.times(16, 16))
                    if not (first and u < 2):
                        act.wait_ge(*when(radial_ready, step, 4 * (u - 2) + 3, each=4))
                    nc.scalar.activation(hidT[0:HID0, u % 2, :, :],
                                         ew_row[:, u % 2, :].rearrange("c (p j) -> c j p", j=TPG),
                                         ACT.Relu, bias=b1c[:, :], scale=w1c[:, :]).then_inc(hid_ready[u], 1)
                    act.wait_ge(gathered[u], step.times(16 * TPG, 16 * TPG))
                    if not (first and u < 2):
                        act.wait_ge(*when(prods_done, step, 4 * (u - 2) + 3, each=4))
                    vec = rows[:, u, :, MUL:F].rearrange("p t (v i) -> p t i v", i=3)
                    nc.scalar.copy(featV[:, u % 2, :, 0:3, 0:MUL], vec)
                    nc.scalar.copy(vectors[:, u % 2, :, 0:3, :], vec)
                    nc.scalar.copy(vectors[:, u % 2, :, 3:5, :], vec[:, :, 0:2, :])
                    nc.scalar.copy(featS[:, u % 2, :, 0:MUL], rows[:, u, :, 0:MUL]).then_inc(rows_copied[u], 1)
                    make_onehot(0, step, u, first)

            root(1, var[:, :])
            root(2, length[:, :])
            act.wait_ge(consts_in, 64)
            act.wait_ge(made, 7)
            act.wait_ge(prepared, 1)
            sweep(act, layer0)
            root(3, dis[:, :])
            root(4, var[:, :])
            for c, at, w in chunks:
                act.wait_ge(feat_turned, c + 1)
                nc.scalar.copy(accT[0:F, at:at + w], radial[1][0:F, c % 2, 0:w]).then_inc(acc_set, 1)
            for c, at, w in chunks:
                act.wait_ge(norm_spread, c + 1)
                nc.scalar.copy(norm_row[:, at:at + w], radial[0][:, c % 2, 0:w]).then_inc(norm_set, 1)

            def conv(n):
                sweep(act, lambda step, first, last: [make_onehot(n, step, u, first) for u in range(UNROLL)])

            def post(k):
                width = HID if k == 0 else F

                def relu(c, at, w):
                    act.wait_ge(scaled[k], c + 1)
                    if c >= 2:
                        act.wait_ge(next_set[0] if k == 0 else projected, c - 1)
                    nc.scalar.activation(rbuf[:, c % 2, 0:w], ybuf[:, c % 2, 0:w], ACT.Relu,
                                         bias=(B1c if k == 0 else B2c)[:, :]).then_inc(relued[k], 1)

                relu(*chunks[0])
                for c, at, w in chunks:
                    if c + 1 < NCH:
                        relu(*chunks[c + 1])
                    act.wait_ge(next_turned[k], c + 1)
                    if c >= 2:
                        act.wait_ge(table_out[k + 2] if c % 2 == 0 else table_odd_out[k], 16 * (c // 2))
                    used = w // P * width
                    nc.scalar.copy(tbuf[:, c % 2, 0:used], radial[1][:, c % 2, 0:used]).then_inc(next_copied[k], 1)

            conv(1)
            act.wait_ge(convs_in, 96)
            post(0)
            conv(2)
            post(1)
            conv(3)

        @block.vector
        def _(dve):
            v = nc.vector
            chain = [0]

            def link(ins):
                chain[0] += 1
                ins.then_inc(v_chain, 1)
                dve.wait_ge(v_chain, chain[0])

            roots = [0]

            def reciprocal_root(ap):
                roots[0] += 1
                v.memset(flag[:, :], 0.0).then_inc(root_asked, 1)
                dve.wait_ge(root_done, roots[0])
                link(v.reciprocal(ap, ap))

            def layernorm(src_ap, dst_ap, tmp_ap):
                link(v.tensor_reduce(mu[:, :], src_ap, X, ALU.add))
                link(v.tensor_scalar(mu[:, :], mu[:, :], 1.0 / F, None, ALU.mult))
                link(v.tensor_tensor(dst_ap, src_ap, mu[:, :].unsqueeze(2).to_broadcast([P, NB, F]), ALU.subtract))
                link(v.tensor_tensor(tmp_ap, dst_ap, dst_ap, ALU.mult))
                link(v.tensor_reduce(var[:, :], tmp_ap, X, ALU.add))
                link(v.tensor_scalar(var[:, :], var[:, :], 1.0 / F, EPS, ALU.mult, ALU.add))
                reciprocal_root(var[:, :])
                link(v.scalar_tensor_tensor(dst_ap, dst_ap, 0.0, var[:, :].unsqueeze(2).to_broadcast([P, NB, F]),
                                            ALU.max, ALU.mult))

            dve.wait_ge(x_in, 16)
            dve.wait_ge(x_tail, 16)
            layernorm(xn[:, :, :], lnA, lnB)
            link(v.memset(nodes[:, :], 0.0))
            v.memset(nodesX[:, :], 0.0).then_inc(table_ready[0], 1)

            dve.wait_ge(rows_in, 48)
            link(v.tensor_reduce(span_i[:, :, 0], dst_rows, X, ALU.min))
            link(v.tensor_reduce(span_i[:, :, 1], dst_rows, X, ALU.max))
            link(v.tensor_copy(meta_i[:, :, 0], span_i[:, :, 0]))
            link(v.tensor_tensor(span_i[:, :, 1], span_i[:, :, 1], span_i[:, :, 0], ALU.subtract))
            v.tensor_scalar(meta_i[:, :, 1], span_i[:, :, 1], WIN.bit_length() - 1, None,
                            ALU.arith_shift_right).then_inc(meta_ready, 1)
            dve.wait_ge(made, 7)
            v.tensor_copy(iota[:, :], iota_i[:, :]).then_inc(meta_ready, 1)
            link(v.tensor_copy(far_shift[:, :], far_shift_i[:, :]))
            dve.wait_ge(meta_ready, 2)
            dve.wait_ge(consts_in, 64)
            wA = w2n[:, 0:256].rearrange("k (m u g v) -> k m u g v", m=2, u=MUL, g=2)
            wB = w2n[:, 256:384].rearrange("k (u m v) -> k u m v", u=MUL, m=2)
            raw = [w2raw[:, n * 64:(n + 1) * 64].rearrange("k (u v) -> k u v", v=MUL) for n in range(3)]
            raw11 = w2raw[:, 192:384].rearrange("k (u v m) -> k u v m", u=MUL, v=MUL)
            link(v.tensor_scalar(wA[:, 1, :, 0, :], raw[0], K00, None, ALU.mult))
            link(v.tensor_scalar(wA[:, 1, :, 1, :], raw[1], K01, None, ALU.mult))
            link(v.tensor_scalar(wA[:, 0, :, 0, :], raw[2], K10, None, ALU.mult))
            link(v.tensor_scalar(wA[:, 0, :, 1, :], raw11[:, :, :, 2], K11_2, None, ALU.mult))
            link(v.tensor_scalar(wB[:, :, 1, :], raw11[:, :, :, 1], K11_1, None, ALU.mult))
            link(v.tensor_scalar(w2raw[:, 0:64], w2raw[:, 192:384].rearrange("k (n m) -> k n m", m=3)[:, :, 2],
                                 -K11_2 / 3, None, ALU.mult))
            link(v.tensor_scalar(w2raw[:, 64:128], w2raw[:, 192:384].rearrange("k (n m) -> k n m", m=3)[:, :, 0],
                                 K11_0, None, ALU.mult))
            link(v.tensor_tensor(wB[:, :, 0, :], raw[0], raw[1], ALU.add))
            dve.wait_ge(edges_in, 32)
            dve.wait_ge(edges_tail, 32)
            dve.wait_ge(meta_in, 16)
            start_all = meta[:, :].rearrange("p (g c) -> p g c", c=2)[:, :, 0:1].to_broadcast([P, NG, TPG])
            link(v.tensor_tensor(rel[:, :].rearrange("p (g j) -> p g j", j=TPG),
                                 dst_i.rearrange("p (g j) -> p g j", j=TPG), start_all, ALU.subtract))
            dve.wait_ge(table_out[0], 16)
            link(v.tensor_tensor(squares, attr, attr, ALU.mult))
            link(v.tensor_reduce(length[:, :], squares, X, ALU.add))
            reciprocal_root(length[:, :])
            inv = length[:, :].unsqueeze(2)
            link(v.tensor_tensor(direction[:, :, 0:2], attr[:, :, 1:3], inv.to_broadcast([P, NG * TPG, 2]), ALU.mult))
            link(v.tensor_tensor(direction[:, :, 2:5], attr, inv.to_broadcast([P, NG * TPG, 3]), ALU.mult))
            link(v.memset(hidT[HID0:HID0 + 1, :, :, :], 1.0))
            by_group = meta[0:1, :].rearrange("p (g c) -> p g c", c=2)
            link(v.memset(late_starts[:, :], 0))
            link(v.tensor_copy(starts[:, 0:NG], by_group[:, :, 0]))
            link(v.tensor_copy(late_starts[:, 1:NG + 1], by_group[:, :, 0]))
            link(v.tensor_copy(further[:, 0:NG], by_group[:, :, 1]))
            link(v.memset(accT[:, :], 0.0))
            link(v.memset(msg[:, :, :, 16:17], 1.0))
            v.memset(relX[:, :], 0.0).then_inc(prepared, 1)

            far_count = dve.alloc_register("far_count")

            def far_windows(n, step, u, n_far):
                with dve.If(n_far > 0):
                    start = dve.value_load(starts[0:1, bass.ds(step.it * UNROLL + u, 1)], min_val=0, max_val=N - 1)
                    with dve.Fori(1, n_far + 1) as k:
                        dve.reg_add(far_count, far_count, 1)
                        count = dve.snap(far_count)
                        v.tensor_scalar(relX[:, :], rel[:, bass.ds(step.it * (UNROLL * TPG) + u * TPG, TPG)], far_shift[:, bass.ds(k, 1)],
                                        None, ALU.subtract).then_inc(far_rel[n], 1)
                        dve.wait_ge(far_rel[n], count)
                        v.tensor_tensor(onehotX[:, :, :], iota[:, :].unsqueeze(1).to_broadcast([P, TPG, WIN]),
                                        relX[:, :].unsqueeze(2).to_broadcast([P, TPG, WIN]),
                                        ALU.is_equal).then_inc(far_onehot[n], 1)
                        dve.wait_ge(far_summed[n], count)
                        first_node = nc.s_assert_within(
                            start + k * WIN, 0, N - 1, skip_runtime_bounds_check_because=
                            "a window starts at or below its group's greatest destination")
                        at = bass.ds(first_node, WIN)
                        if n == 0:
                            v.tensor_copy(nodesX[:, 0:MUL + 1], psX[:, 0:MUL + 1])
                            v.tensor_reduce(nodesX[:, MUL + 1:F + 1],
                                            psX[:, MUL + 1:SEGW].rearrange("p (c s) -> p c s", s=16),
                                            X, ALU.add).then_inc(far_nodes, 1)
                            dve.wait_ge(far_turned, count)
                            v.tensor_tensor(accT[0:F + 1, at], accT[0:F + 1, at], psT[0:F + 1, 0:WIN],
                                            ALU.add).then_inc(far_added[n], 1)
                        else:
                            w = WIDTH[n]
                            v.tensor_tensor(accT[0:w, at], accT[0:w, at], psX[0:w, 0:WIN],
                                            ALU.add).then_inc(far_added[n], 1)
                        dve.wait_ge(far_added[n], count)

            shapeV = [P, TPG, 3, MUL]

            def along_parts(step, u):
                s, d = u % 2, direction[:, bass.ds(step.tile(u), TPG), :]
                dve.wait_ge(*when(rows_copied, step, u))
                v.tensor_tensor(dotp[:, :, :, :], vectors[:, s, :, 0:3, :],
                                d[:, :, 0:3].unsqueeze(3).to_broadcast(shapeV), ALU.mult).then_inc(dot_ready[u % 2], 1)

            def cross_parts(step, u):
                s, d = u % 2, direction[:, bass.ds(step.tile(u), TPG), :]
                v.tensor_tensor(cross1[:, :, :, :], vectors[:, s, :, 2:5, :],
                                d[:, :, 1:4].unsqueeze(3).to_broadcast(shapeV), ALU.mult)
                v.tensor_tensor(cross2[:, :, :, :], vectors[:, s, :, 1:4, :],
                                d[:, :, 2:5].unsqueeze(3).to_broadcast(shapeV), ALU.mult).then_inc(cross_ready[u % UNROLL], 1)

            def feature_along(step, u):
                dve.wait_ge(*when(dot_ready, step, u))
                v.tensor_reduce(featS[:, u % 2, :, MUL:2 * MUL],
                                dotp[:, :, :, :].rearrange("p t i v -> p t v i"),
                                X, ALU.add).then_inc(feat_along_ready[u % 2], 1)

            def feature_cross(step, u):
                dve.wait_ge(*when(cross_ready, step, u))
                v.tensor_tensor(featV[:, u % 2, :, 0:3, MUL:2 * MUL], cross1[:, :, :, :], cross2[:, :, :, :],
                                ALU.subtract).then_inc(feats_ready[u % UNROLL], 1)

            def products(step, u, h, first):
                s = u % 2
                if not (first and u == 0):
                    dve.wait_ge(*when(half_summed, step, 2 * (u - 1) + h, each=2))
                for q in range(2):
                    dve.wait_ge(*when(radial_ready, step, 4 * u + 2 * h + q, each=4))
                    if h == 0 and q == 0:
                        dve.wait_ge(*when(feat_along_ready, step, u))
                    R = radial[q]
                    t = 2 * q
                    prod = v.tensor_tensor(
                        prodA[:, h, t:t + 2, :].rearrange("p t (m s) -> p t m s", s=16),
                        R[:, :, 0:256].rearrange("p t (m s) -> p t m s", s=16),
                        featS[:, s, 4 * h + t:4 * h + t + 2, :].unsqueeze(2).to_broadcast([P, 2, 16, 16]), ALU.mult)
                    if q == 1:
                        prod.then_inc(scalar_prods[(2 * u + h) % 4], 1)
                    elif h == 0:
                        dve.wait_ge(*when(feats_ready, step, u))
                    last = v.tensor_tensor(
                        msg[:, h, t:t + 2, 17:401].rearrange("p t (i u s) -> p t i (u s)", i=3, u=MUL),
                        R[:, :, 256:384].unsqueeze(2).to_broadcast([P, 2, 3, 128]),
                        featV[:, s, 4 * h + t:4 * h + t + 2, :, :].rearrange("p t i s -> p (t i) s").unsqueeze(2)
                        .to_broadcast([P, 6, MUL, 16]), ALU.mult)
                    last.then_inc(prods_done[(4 * u + 2 * h + q) % 8], 1)

            def scalar_sums(step, u, h):
                dve.wait_ge(*when(scalar_prods, step, 2 * u + h, each=2))
                v.tensor_reduce(msg[:, h, :, 0:16], prodA[:, h, :, :].rearrange("p t (m s) -> p t m s", s=16),
                                X, ALU.add).then_inc(scalars_ready[(2 * u + h) % 4], 1)

            def direction_part(step, u, h):
                dve.wait_ge(*when(scalars_ready, step, 2 * u + h, each=2))
                v.tensor_tensor(along[:, :, :, :], msg[:, h, :, 0:MUL].unsqueeze(2).to_broadcast([P, 4, 3, MUL]),
                                direction[:, bass.ds(step.tile(u) + 4 * h, 4), 0:3].unsqueeze(3)
                                .to_broadcast([P, 4, 3, MUL]),
                                ALU.mult).then_inc(along_ready[(2 * u + h) % 4], 1)

            def add_direction_part(step, u, h):
                dve.wait_ge(*when(along_ready, step, 2 * u + h, each=2))
                slot = msg[:, h, :, 17:401].rearrange("p t (n s) -> p t n s", s=16)[:, :, :, 0]
                v.tensor_tensor(slot, slot, along[:, :, :, :].rearrange("p t o u -> p t (o u)"),
                                ALU.add).then_inc(msg_ready[(2 * u + h) % 4], 1)

            def window_sums(step, u):
                dve.wait_ge(*when(half_summed, step, 2 * u + 1, each=2))
                v.tensor_copy(nodes[:, 0:MUL + 1], sums[:, u % 2, 0:MUL + 1])
                v.tensor_reduce(nodes[:, MUL + 1:F + 1],
                                sums[:, u % 2, MUL + 1:SEGW].rearrange("p (c s) -> p c s", s=16),
                                X, ALU.add).then_inc(nodes_ready[u % UNROLL], 1)

            def window_add(step, u, start, first):
                dve.wait_ge(*when(nodes_turned, step, u))
                if not (first and u == 0):
                    dve.wait_ge(*when(added, step, u - 1))
                window = bass.ds(start, WIN)
                v.tensor_tensor(accT[0:F + 1, window], accT[0:F + 1, window], psT[0:F + 1, 0:WIN],
                                ALU.add).then_inc(added[u % UNROLL], 1)

            def load_registers(table, step, top):
                return nc.values_load_multi_w_load_instructions(
                    table[0:1, bass.ds(step.times(UNROLL, 0), UNROLL)], [dve.engine], min_val=0, max_val=top,
                    skip_runtime_bounds_check_because=IN_RANGE)[1]

            def layer0(step, first, last):
                for u in range(UNROLL):
                    before = not (first and u == 0)
                    after = not (last and u == UNROLL - 1)
                    products(step, u, 0, first)
                    if u == 0:
                        late_start = load_registers(late_starts, step, N - 1)
                        n_far = load_registers(further, step, NB)
                    scalar_sums(step, u, 0)
                    if before:
                        window_sums(step, u - 1)
                    direction_part(step, u, 0)
                    if after:
                        along_parts(step, u + 1)
                    add_direction_part(step, u, 0)
                    products(step, u, 1, first)
                    scalar_sums(step, u, 1)
                    if after:
                        cross_parts(step, u + 1)
                    direction_part(step, u, 1)
                    if before:
                        window_add(step, u - 1, late_start[u], first)
                    add_direction_part(step, u, 1)
                    far_windows(0, step, u, n_far[u])
                    if after:
                        feature_along(step, u + 1)
                        feature_cross(step, u + 1)

            dve.reg_mov(far_count, 0)
            along_parts(first_step, 0)
            cross_parts(first_step, 0)
            feature_along(first_step, 0)
            feature_cross(first_step, 0)
            sweep(dve, layer0)
            window_sums(last_step, UNROLL - 1)
            window_add(last_step, UNROLL - 1,
                       dve.value_load(starts[0:1, NG - 1:NG], min_val=0, max_val=N - 1), False)

            for k in range(NTB):
                dve.wait_ge(blocks_turned, k + 1)
                bs = slice(k * TB, (k + 1) * TB)
                ps = radial[0][:, k % 2, 0:TB * (F + 1)].rearrange("p (b c) -> p b c", c=F + 1)
                v.tensor_tensor(xn[:, bs, 0:MUL], xn[:, bs, 0:MUL], ps[:, :, 0:MUL], ALU.add)
                xv = xn[:, bs, MUL:F].rearrange("p b (u o) -> p b o u", o=3)
                v.tensor_tensor(xv, xv, ps[:, :, MUL + 1:F + 1].rearrange("p b (o u) -> p b o u", o=3), ALU.add)
                v.tensor_scalar(dis[:, bs], ps[:, :, MUL], 1.0, None, ALU.add).then_inc(blocks_read, 1)
            dve.wait_ge(blocks_read, NTB)
            reciprocal_root(dis[:, :])
            layernorm(xn[:, :, :], lnA, lnB)
            v.tensor_tensor(lnA, lnA, dis[:, :].unsqueeze(2).to_broadcast([P, NB, F]),
                            ALU.mult).then_inc(table_ready[1], 1)

            def conv(n):
                w = WIDTH[n]

                def body(step, first, last):
                    start = load_registers(starts, step, N - 1)
                    n_far = load_registers(further, step, NB)
                    for u in range(UNROLL):
                        far_windows(n, step, u, n_far[u])
                        dve.wait_ge(*when(group_summed, step, u, layer=n - 1))
                        dve.wait_ge(*when(added, step, u - 1, layer=n))
                        window = bass.ds(start[u], WIN)
                        v.tensor_tensor(accT[0:w, window], accT[0:w, window], sums[0:w, u % 2, 0:WIN],
                                        ALU.add).then_inc(added[u], 1)
                dve.reg_mov(far_count, 0)
                sweep(dve, body)

            def post(k):
                def scale(c, at, w):
                    dve.wait_ge(mm_done[k], c + 1)
                    if c >= 2:
                        dve.wait_ge(relued[k], c - 1)
                    v.tensor_tensor(ybuf[:, c % 2, 0:w], radial[0][:, c % 2, 0:w], norm_row[:, at:at + w],
                                    ALU.mult).then_inc(scaled[k], 1)

                scale(*chunks[0])
                for c, at, w in chunks:
                    if c + 1 < NCH:
                        scale(*chunks[c + 1])
                    if k == 0:
                        dve.wait_ge(relued[k], c + 1)
                        v.tensor_tensor(accT[:, at:at + w], rbuf[:, c % 2, 0:w], norm_row[:, at:at + w],
                                        ALU.mult).then_inc(next_set[k], 1)
                    else:
                        dve.wait_ge(projected, c + 1)
                        v.tensor_tensor(accT[0:F, at:at + w], sums[0:F, c % 2, 0:w], norm_row[0:F, at:at + w],
                                        ALU.mult).then_inc(next_set[k], 1)
                dve.wait_ge(next_set[k], NCH)

            dve.wait_ge(acc_set, NCH)
            conv(1)
            dve.wait_ge(norm_set, NCH)
            post(0)
            conv(2)
            post(1)
            conv(3)

            dve.wait_ge(convs_in, 96)
            for k in range(NTB):
                dve.wait_ge(out_turned, k + 1)
                bs = slice(k * TB, (k + 1) * TB)
                ps = radial[0][:, k % 2, 0:TB * F].rearrange("p (b c) -> p b c", c=F)
                link(v.tensor_tensor(lnA[:, bs, :], ps, dis[:, bs].unsqueeze(2).to_broadcast([P, TB, F]), ALU.mult))
                link(v.tensor_tensor(lnA[:, bs, :], lnA[:, bs, :], B3r[:, :].unsqueeze(1).to_broadcast([P, TB, F]),
                                     ALU.add))
                v.scalar_tensor_tensor(lnA[:, bs, :], lnA[:, bs, :], 0.0, xn[:, bs, :],
                                       ALU.max, ALU.add).then_inc(out_ready, 1)

        @block.tensor
        def _(pe):
            far_count = pe.alloc_register("far_count_pe")
            turn = [pe.alloc_register(f"turn_pe{u}") for u in range(UNROLL)]

            def load_further(step):
                return nc.values_load_multi_w_load_instructions(
                    further[0:1, bass.ds(step.times(UNROLL, 0), UNROLL)], [pe.engine], min_val=0, max_val=NB,
                    skip_runtime_bounds_check_because=IN_RANGE)[1]

            def far_windows(n, n_far):
                with pe.If(n_far > 0):
                    with pe.Fori(1, n_far + 1):
                        count = pe.snap(far_count) + 1
                        pe.wait_ge(far_onehot[n], count)
                        for j in range(TPG):
                            if n == 0:
                                last = nc.tensor.matmul(psX[:, 0:SEGW], onehotX[:, j, :],
                                                        msg[:, j // 4, j % 4, MUL:MUL + SEGW],
                                                        start=(j == 0), stop=(j == TPG - 1))
                            else:
                                last = nc.tensor.matmul(psX[0:WIDTH[n], 0:WIN], far_rows[j], onehotX[:, j, :],
                                                        start=(j == 0), stop=(j == TPG - 1))
                        last.then_inc(far_summed[n], 1)
                        if n == 0:
                            pe.wait_ge(far_nodes, count)
                            pe.reg_add(far_count, far_count, 1)
                            nc.tensor.transpose(psT[0:F + 1, 0:P], nodesX[:, :], ident[:, :]).then_inc(far_turned, 1)
                        else:
                            pe.reg_add(far_count, far_count, 1)

            def radial_pair(step, u, q, free=True):
                if q == 0:
                    pe.wait_ge(*when(hid_ready, step, u))
                if free:
                    pe.wait_ge(*when(prods_done, step, 4 * u + q - 2, each=4))
                for k in range(2):
                    last = nc.tensor.matmul(radial[q % 2][:, k, 0:RDIM], hidT[:, u % 2, 2 * q + k, :], w2n[:, :],
                                            start=True, stop=True)
                last.then_inc(radial_ready[(4 * u + q) % 8], 1)

            def sum_half(step, u, h, first):
                pe.wait_ge(*when(msg_ready, step, 2 * u + h, each=2))
                if h == 0:
                    pe.wait_ge(*when(onehot_ready, step, u))
                    if not (first and u < 2):
                        pe.wait_ge(*when(nodes_ready, step, u - 2))
                for k in range(4):
                    last = nc.tensor.matmul(sums[:, u % 2, 0:SEGW], onehot[:, u % 2, 4 * h + k, :],
                                            msg[:, h, k, MUL:MUL + SEGW],
                                            start=(h == 0 and k == 0), stop=(h == 1 and k == 3))
                last.then_inc(half_summed[(2 * u + h) % 4], 1)

            def turn_nodes(step, u, first):
                r = u % UNROLL
                now = step.it if step.peeled else pe.snap(turn[r]) + 1
                pe.wait_ge(nodes_ready[r], now + (1 if u >= 0 else 0))
                if not (first and u == 0):
                    pe.wait_ge(*when(added, step, u - 1))
                if not step.peeled:
                    pe.reg_add(turn[r], turn[r], 1)
                nc.tensor.transpose(psT[0:F + 1, 0:P], nodes[:, :], ident[:, :]).then_inc(nodes_turned[r], 1)

            def layer0(step, first, last):
                for u in range(UNROLL):
                    radial_pair(step, u, 2)
                    if u == 0:
                        n_far = load_further(step)
                    radial_pair(step, u, 3)
                    sum_half(step, u, 0, first)
                    if not (first and u == 0):
                        turn_nodes(step, u - 1, first)
                    if not (last and u == UNROLL - 1):
                        radial_pair(step, u + 1, 0)
                        radial_pair(step, u + 1, 1)
                    sum_half(step, u, 1, first)
                    far_windows(0, n_far[u])

            pe.wait_ge(made, 7)
            pe.wait_ge(prepared, 1)
            pe.wait_ge(meta_in, 16)
            pe.reg_mov(far_count, 0)
            for u in range(UNROLL):
                pe.reg_mov(turn[u], 0)
            radial_pair(first_step, 0, 0, False)
            radial_pair(first_step, 0, 1, False)
            sweep(pe, layer0)
            turn_nodes(last_step, UNROLL - 1, False)

            pe.wait_ge(*when(added, last_step, UNROLL - 1))
            for k in range(NTB):
                if k >= 2:
                    pe.wait_ge(blocks_read, k - 1)
                for j in range(TB):
                    at = (k * TB + j) * P
                    last = nc.tensor.transpose(radial[0][:, k % 2, j * (F + 1):(j + 1) * (F + 1)],
                                               accT[0:F + 1, at:at + P], ident[0:F + 1, 0:F + 1])
                last.then_inc(blocks_turned, 1)
            pe.wait_ge(table_ready[1], 1)
            for c, at, w in chunks:
                if c >= 2:
                    pe.wait_ge(acc_set, c - 1)
                for j in range(w // P):
                    last = nc.tensor.transpose(radial[1][0:F, c % 2, j * P:(j + 1) * P],
                                               lnA[:, c * CH + j, :], ident[:, :])
                last.then_inc(feat_turned, 1)
            for c, at, w in chunks:
                if c >= 2:
                    pe.wait_ge(norm_set, c - 1)
                for j in range(w // P):
                    b = c * CH + j
                    last = nc.tensor.matmul(radial[0][:, c % 2, j * P:(j + 1) * P],
                                            dis[:, b:b + 1].to_broadcast([P, P]), ident[:, :],
                                            start=True, stop=True)
                last.then_inc(norm_spread, 1)

            def conv(n):
                w = WIDTH[n]

                def body(step, first, last):
                    n_far = load_further(step)
                    for u in range(UNROLL):
                        pe.wait_ge(gathered[u], step.times(16 * TPG, (n * NIT + 1) * (16 * TPG)))
                        pe.wait_ge(*when(onehot_ready, step, u, layer=n))
                        pe.wait_ge(*when(added, step, u - 2, layer=n))
                        for j in range(TPG):
                            mm = nc.tensor.matmul(sums[0:w, u % 2, 0:WIN], rows[:, u, j, 0:w],
                                                  onehot[:, u % 2, j, :], start=(j == 0), stop=(j == TPG - 1))
                        mm.then_inc(group_summed[u], 1)
                        for j in range(TPG):
                            far_rows[j] = rows[:, u, j, 0:w]
                        far_windows(n, n_far[u])
                pe.reg_mov(far_count, 0)
                sweep(pe, body)

            def post(k):
                width = HID if k == 0 else F
                rows_in_acc = F if k == 0 else HID

                def weigh(c, at, w):
                    if c >= 2:
                        pe.wait_ge(scaled[k], c - 1)
                    nc.tensor.matmul(radial[0][:, c % 2, 0:w], (W1s if k == 0 else W2s)[:, :],
                                     accT[0:rows_in_acc, at:at + w], start=True, stop=True).then_inc(mm_done[k], 1)

                pe.wait_ge(*when(added, last_step, UNROLL - 1, layer=k + 1))
                weigh(*chunks[0])
                for c, at, w in chunks:
                    if c + 1 < NCH:
                        weigh(*chunks[c + 1])
                    if k == 1:
                        pe.wait_ge(relued[k], c + 1)
                        if c >= 2:
                            pe.wait_ge(next_set[k], c - 1)
                        nc.tensor.matmul(sums[0:F, c % 2, 0:w], W3s[:, :], rbuf[:, c % 2, 0:w],
                                         start=True, stop=True).then_inc(projected, 1)
                    pe.wait_ge(next_set[k], c + 1)
                    if c >= 2:
                        pe.wait_ge(next_copied[k], c - 1)
                    for j in range(w // P):
                        last = nc.tensor.transpose(radial[1][:, c % 2, j * width:(j + 1) * width],
                                                   accT[0:width, at + j * P:at + (j + 1) * P],
                                                   ident[0:width, 0:width])
                    last.then_inc(next_turned[k], 1)

            far_rows = [None] * TPG
            conv(1)
            pe.wait_ge(convs_in, 96)
            post(0)
            conv(2)
            post(1)
            conv(3)
            pe.wait_ge(*when(added, last_step, UNROLL - 1, layer=NLAYER - 1))
            for k in range(NTB):
                if k >= 2:
                    pe.wait_ge(out_ready, k - 1)
                for j in range(TB):
                    at = (k * TB + j) * P
                    last = nc.tensor.transpose(radial[0][:, k % 2, j * F:(j + 1) * F],
                                               accT[0:F, at:at + P], ident[0:F, 0:F])
                last.then_inc(out_turned, 1)


_INS = ["x", "src", "dst", "edge_attr_3", "edge_weight", "L0_gnn_w1", "L0_gnn_b1", "L0_gnn_w2", "L0_gnn_b2",
        "L1_gnn_W1", "L1_gnn_b1", "L1_gnn_W2", "L1_gnn_b2", "L1_gnn_W3", "L1_gnn_b3"]


def kernel(**inputs):
    import numpy as np
    import concourse.bacc as bacc
    from concourse.bass_utils import run_bass_kernel_spmd

    nc = bacc.Bacc("TRN2", target_bir_lowering=False, num_devices=1)
    arrays, args = {}, []
    for name in _INS:
        a = np.ascontiguousarray(inputs[name])
        arrays[f"in_{name}"] = a
        args.append(nc.dram_tensor(f"in_{name}", a.shape, mybir.dt.from_np(a.dtype), kind="ExternalInput").ap())
    args.append(nc.dram_tensor("out", (N, F), fp32, kind="ExternalOutput").ap())
    gnn_kernel(nc, *args)
    r = run_bass_kernel_spmd(nc, [arrays], core_ids=[0])
    return r.results[0]["out"]
```

```python
import concourse.bass as bass
from concourse import mybir
from contextlib import ExitStack
from math import pi, sqrt

P = 128
N = 12500
E = 200000
F = 32
MUL = 8
NB = -(-N // P)
NPAD = NB * P
NTAIL = N - (NB - 1) * P
TPG = 8
GE = TPG * P
NG = -(-E // GE)
UNROLL = 4
NIT = NG // UNROLL
ETAIL = E - (NG - 1) * GE
TTAIL = 4
PTAIL = ETAIL // TTAIL
WIN = 128
RDIM = 6 * MUL * MUL
HID0 = 64
HID = 128
NLAYER = 4
WIDTH = [F, F, HID, F]
EPS = 1e-5
SEGW = MUL + 1 + 24 * 16
assert NG % UNROLL == 0 and PTAIL * TTAIL == ETAIL and PTAIL <= P

NORM0 = sqrt(4 * pi) / sqrt(2 * MUL)
NORM1 = sqrt(4 * pi) * sqrt(3) / sqrt(4 * MUL)
Y0 = 0.5 / sqrt(pi)
Y1 = sqrt(3 / (4 * pi))
K00 = NORM0 * Y0
K01 = NORM0 * Y1 / sqrt(3)
K10 = NORM1 * Y1 / sqrt(3)
K11_0 = NORM1 * Y0 / sqrt(3)
K11_1 = NORM1 * Y1 / sqrt(6)
K11_2 = NORM1 * sqrt(3 / (8 * pi))

IN_RANGE = "the tables hold least destinations, in [0, N), and (greatest - least) / 128, below NB"

fp32 = mybir.dt.float32
i32 = mybir.dt.int32
ALU = mybir.AluOpType
ACT = mybir.ActivationFunctionType
X = mybir.AxisListType.X


def gnn_kernel(nc, x, src, dst, edge_attr, edge_weight, w1, b1, w2, b2,
               W1, B1, W2, B2, W3, B3, out):
    ctx = ExitStack()
    with ctx:
        def sb(name, shape, dt=fp32):
            return ctx.enter_context(nc.sbuf_tensor(name, shape, dt))

        def pb(name, shape, dt=fp32):
            return ctx.enter_context(nc.psum_tensor(name, shape, dt))

        def sem(name):
            return ctx.enter_context(nc.semaphore(name))

        tables = [nc.dram_tensor(f"table{n}", [NPAD, WIDTH[n]], fp32, kind="Internal").ap()
                  for n in range(NLAYER)]
        norm_d = nc.dram_tensor("norm_d", [NB, P], fp32, kind="Internal").ap()
        meta_d = nc.dram_tensor("meta_d", [NG, 2], i32, kind="Internal").ap()

        accT = sb("accT", [P, NPAD + WIN])
        arena = sb("arena", [P, NPAD])
        direction = arena[:, 0:NG * TPG * 5].rearrange("p (t c) -> p t c", c=5)
        squares = arena[:, NG * TPG * 5:NG * TPG * 8].rearrange("p (t c) -> p t c", c=3)
        norm_row = arena[:, :]
        xn = sb("xn", [P, NB, F])
        scratch = sb("scratch", [P, 2 * NB * F])
        msg = scratch[:, 0:2 * 4 * 401].rearrange("p (h t c) -> p h t c", h=2, t=4)
        prodA = scratch[:, 3208:3208 + 2 * 4 * 256].rearrange("p (h t c) -> p h t c", h=2, t=4)
        lnA = scratch[:, 0:NB * F].rearrange("p (b f) -> p b f", f=F)
        lnB = scratch[:, NB * F:2 * NB * F].rearrange("p (b f) -> p b f", f=F)
        ybuf = scratch[:, NB * F:NB * F + 1024].rearrange("p (s n) -> p s n", s=2)
        rbuf = scratch[:, NB * F + 1024:NB * F + 2048].rearrange("p (s n) -> p s n", s=2)
        table2 = arena[:, :].rearrange("p (b f) -> p b f", f=HID)
        length = scratch[:, NG * TPG * 3:NG * TPG * 4]
        dst_rows = accT[0:NB, 0:2 * GE].bitcast(i32).rearrange("p (h e) -> p h e", h=2)
        dst_i = accT[:, 2048:2048 + NG * TPG].bitcast(i32)
        attr = accT[:, 4096:4096 + NG * TPG * 3].rearrange("p (t c) -> p t c", c=3)
        iota_i = accT[:, 9000:9000 + WIN].bitcast(i32)
        far_shift_i = accT[:, 9200:9200 + NB + 1].bitcast(i32)
        w2raw = accT[0:HID0 + 1, 9400:9400 + RDIM]
        meta = accT[:, 10000:10000 + NG * 2].bitcast(i32)
        rel = sb("rel", [P, NG * TPG])
        idx = sb("idx", [P, UNROLL, TPG], i32)
        rows = sb("rows", [P, UNROLL, TPG, HID])
        ew_row = sb("ew_row", [HID0, 2, GE])
        hidT = sb("hidT", [HID0 + 1, 2, TPG, P])
        onehot = sb("onehot", [P, 2, TPG, WIN])
        dist = sb("dist", [P, TPG, WIN])
        onehotX = sb("onehotX", [P, TPG, WIN])
        relX = sb("relX", [P, TPG])
        featV = sb("featV", [P, 2, TPG, 3, 16])
        vectors = arena[:, 8000:8000 + 2 * TPG * 5 * MUL].rearrange(
            "p (s t i v) -> p s t i v", s=2, t=TPG, i=5)
        featS = sb("featS", [P, 2, TPG, 16])
        dotp = sb("dotp", [P, TPG, 3, MUL])
        cross1 = sb("cross1", [P, TPG, 3, MUL])
        cross2 = sb("cross2", [P, TPG, 3, MUL])
        along = sb("along", [P, 4, 3, MUL])
        nodes = sb("nodes", [P, F + 1])
        nodesX = sb("nodesX", [P, F + 1])
        mu = sb("mu", [P, NB])
        var = sb("var", [P, NB])
        dis = sb("dis", [P, NB])
        dis2 = sb("dis2", [P, NB])
        norm_cols = sb("norm_cols", [NB, P])
        meta_i = sb("meta_i", [NB, 2, 2], i32)
        span_i = sb("span_i", [NB, 2, 2], i32)
        starts = sb("starts", [1, NG + 4], i32)
        late_starts = sb("late_starts", [1, NG + 4], i32)
        further = sb("further", [1, NG + 4], i32)
        iota = sb("iota", [P, WIN])
        far_shift = sb("far_shift", [P, NB + 1])
        ident = sb("ident", [P, P])
        one = sb("one", [P, 1])
        flag = sb("flag", [P, 1])
        w1c = sb("w1c", [HID0, 1])
        b1c = sb("b1c", [HID0, 1])
        w2n = sb("w2n", [HID0 + 1, RDIM])
        W1s = sb("W1s", [F + 1, HID])
        W2s = sb("W2s", [HID, HID])
        W3s = sb("W3s", [HID, F])
        B2c = sb("B2c", [HID, 1])
        B3r = sb("B3r", [P, F])

        radial = [pb(f"radial{i}", [P, 2, 512]) for i in range(2)]
        sums = pb("sums", [P, 2, 512])
        psT = pb("psT", [P, 512])
        psX = pb("psX", [P, 512])

        def sems(name, count=UNROLL):
            return [sem(f"{name}{i}") for i in range(count)]

        x_in = sem("x_in")
        x_tail = sem("x_tail")
        edges_in = sem("edges_in")
        edges_tail = sem("edges_tail")
        rows_in = sem("rows_in")
        consts_in = sem("consts_in")
        convs_in = sem("convs_in")
        root_asked = sem("root_asked")
        root_done = sem("root_done")
        made = sem("made")
        pads = sem("pads")
        prepared = sem("prepared")
        squared = sem("squared")
        directed = sem("directed")
        repeated = sem("repeated")
        acc_cleared = sem("acc_cleared")
        v_chain = sem("v_chain")
        meta_out = sem("meta_out")
        meta_in = sem("meta_in")
        meta_ready = sem("meta_ready")
        table_ready = sems("table_ready", 2)
        centred = sem("centred")
        ln_squared = sem("ln_squared")
        table_out = sems("table_out", 2)
        chunk_out = sems("chunk_out", 4)
        idx_in = [sem(f"idx_in{u}") for u in range(UNROLL)]
        gathered = [sem(f"gathered{u}") for u in range(UNROLL)]
        ew_in = sems("ew_in")
        hid_ready = sems("hid_ready")
        rows_copied = sems("rows_copied")
        dist_ready = sems("dist_ready", 2)
        onehot_ready = sems("onehot_ready")
        radial_ready = sems("radial_ready", 8)
        prods_done = sems("prods_done", 8)
        scalar_prods = sems("scalar_prods")
        feat_along_ready = sems("feat_along_ready", 2)
        dot_ready = sems("dot_ready", 2)
        cross_ready = sems("cross_ready", 2)
        feats_ready = sems("feats_ready", 2)
        scalars_ready = sems("scalars_ready")
        along_ready = sems("along_ready")
        msg_ready = sems("msg_ready")
        half_summed = sems("half_summed")
        nodes_ready = sems("nodes_ready")
        nodes_turned = sems("nodes_turned")
        added = sems("added")
        group_summed = sems("group_summed")
        far_rel = [sem(f"far_rel{n}") for n in range(NLAYER)]
        far_onehot = [sem(f"far_onehot{n}") for n in range(NLAYER)]
        far_summed = [sem(f"far_summed{n}") for n in range(NLAYER)]
        far_nodes = sem("far_nodes")
        far_turned = sem("far_turned")
        far_added = [sem(f"far_added{n}") for n in range(NLAYER)]
        blocks_turned = sem("blocks_turned")
        blocks_read = sem("blocks_read")
        feat_turned = sem("feat_turned")
        acc_set = sem("acc_set")
        norm_turned = sem("norm_turned")
        norm_copied = sem("norm_copied")
        norm_out = sem("norm_out")
        norm_in = sem("norm_in")
        counts_moved = sem("counts_moved")
        row_rooted = sem("row_rooted")
        weighed = sems("weighed", 2)
        scaled = sem("scaled")
        relued = sem("relued")
        projected = sem("projected")
        next_set = sems("next_set", 2)
        out_turned = sem("out_turned")
        out_ready = sem("out_ready")
        out_done = sem("out_done")

        block = ctx.enter_context(nc.Block())

        class Step:
            def __init__(self, eng, it):
                self.eng, self.it, self.known = eng, it, {}
                self.peeled = isinstance(it, int)

            def times(self, factor, plus):
                if self.peeled:
                    return self.it * factor + plus
                if (factor, plus) not in self.known:
                    self.known[factor, plus] = self.eng.snap(
                        self.it * factor + plus, min_val=factor + plus, max_val=(NIT - 2) * factor + plus)
                return self.known[factor, plus]

            def tile(self, u):
                return self.times(UNROLL * TPG, u * TPG)

        def when(sems, step, event, each=1, layer=0):
            n = len(sems)
            rounds = UNROLL * each // n
            return sems[event % n], step.times(rounds, layer * NIT * rounds + event // n + 1)

        def rows_gathered(step, u, n, plus, last):
            less = (n + (1 if last and plus else 0)) * (TPG - TTAIL) if u == UNROLL - 1 else 0
            return step.times(16 * TPG, 16 * (TPG * (n * NIT + plus) - less))

        def sweep(eng, body):
            body(Step(eng, 0), True, False)
            with eng.Fori(1, NIT - 1) as it:
                body(Step(eng, it), False, False)
            body(Step(eng, NIT - 1), False, True)

        first_step = Step(None, 0)
        last_step = Step(None, NIT - 1)

        CH = 4
        NCH = -(-NB // CH)
        chunks = [(c, c * CH * P, min(CH * P, NPAD - c * CH * P)) for c in range(NCH)]

        def chunks_stored(n, c):
            return 16 * (c // 4 + 1) + (16 * len(range(c % 4, NCH, 4)) if n == 3 else 0)

        HALVES = [slice(0, NB // 2), slice(NB // 2, NB)]
        TB = 14
        NTB = NB // TB

        @block.sync
        def _(sp):
            sp.dma_start(xn[:, 0:NB - 1, :],
                         x[0:(NB - 1) * P, :].rearrange("(b p) f -> p b f", p=P)).then_inc(x_in, 16)
            sp.dma_start(dst_rows[:, 0, :], dst[0:NB * GE].rearrange("(g e) -> g e", e=GE)).then_inc(rows_in, 16)
            sp.dma_start(dst_rows[0:NB - 1, 1, :],
                         dst[NB * GE:(NG - 1) * GE].rearrange("(g e) -> g e", e=GE)).then_inc(rows_in, 16)
            sp.dma_start(dst_rows[NB - 1:NB, 1, :],
                         dst[E - GE:E].rearrange("(g e) -> g e", e=GE)).then_inc(rows_in, 16)
            sp.wait_ge(pads, 1)
            sp.dma_start(xn[0:NTAIL, NB - 1, :], x[(NB - 1) * P:N, :]).then_inc(x_tail, 16)
            full = (NG - 1) * TPG
            sp.dma_start(dst_i[:, 0:full].rearrange("p (g j) -> p g j", j=TPG),
                         dst[0:(NG - 1) * GE].rearrange("(g p j) -> p g j", p=P, j=TPG)).then_inc(edges_in, 16)
            sp.dma_start(attr[:, 0:full, :].rearrange("p (g j) c -> p g (j c)", j=TPG),
                         edge_attr[0:(NG - 1) * GE, :].rearrange("(g p j) c -> p g (j c)", p=P, j=TPG)).then_inc(edges_in, 16)
            sp.wait_ge(pads, 3)
            sp.dma_start(dst_i[0:PTAIL, full:full + TTAIL],
                         dst[(NG - 1) * GE:E].rearrange("(p j) -> p j", j=TTAIL)).then_inc(edges_tail, 16)
            sp.dma_start(attr[0:PTAIL, full:full + TTAIL, :].rearrange("p j c -> p (j c)"),
                         edge_attr[(NG - 1) * GE:E, :].rearrange("(p j) c -> p (j c)", j=TTAIL)).then_inc(edges_tail, 16)
            sp.wait_ge(meta_ready, 2)
            sp.dma_start(meta_d.rearrange("(h r) c -> r h c", r=NB), meta_i[:, :, :]).then_inc(meta_out, 16)
            sp.wait_ge(meta_out, 16)
            sp.dma_start(meta[:, :], meta_d.rearrange("g c -> (g c)").partition_broadcast(P)).then_inc(meta_in, 16)

            def load_idx(n, step, u, first, last):
                if n > 0 or not first:
                    sp.wait_ge(gathered[u], rows_gathered(step, u, n, 0, False))
                if last and u == UNROLL - 1:
                    d = idx[0:PTAIL, u, 0:TTAIL]
                    s = src[(NG - 1) * GE:E].rearrange("(p j) -> p j", j=TTAIL)
                else:
                    d = idx[:, u, :]
                    s = src[bass.ds(step.times(UNROLL * GE, u * GE), GE)].rearrange("(p j) -> p j", j=TPG)
                sp.dma_start(d, s).then_inc(idx_in[u], 16)

            def load_ew(step, u, first, last):
                if not (first and u < 2):
                    sp.wait_ge(*when(hid_ready, step, u - 2))
                if last and u == UNROLL - 1:
                    d = ew_row[:, u % 2, 0:ETAIL]
                    s = edge_weight[(NG - 1) * GE:E]
                else:
                    d = ew_row[:, u % 2, :]
                    s = edge_weight[bass.ds(step.times(UNROLL * GE, u * GE), GE)]
                sp.dma_start(d, s.partition_broadcast(HID0)).then_inc(ew_in[u], 16)

            def layer0(step, first, last):
                for u in range(UNROLL):
                    load_idx(0, step, u, first, last)
                    load_ew(step, u, first, last)

            def table_halves(n):
                for k, bs in enumerate(HALVES):
                    sp.wait_ge(table_ready[n], k + 1)
                    sp.dma_start(tables[n][bs.start * P:bs.stop * P, :].rearrange("(b p) f -> p b f", p=P),
                                 lnA[:, bs, :]).then_inc(table_out[n], 16)

            def table_chunks(n, view_of):
                for c, at, w in chunks:
                    sp.wait_ge(next_set[n - 2], c + 1)
                    if n == 3 or c >= 4:
                        sp.wait_ge(chunk_out[c % 4], chunks_stored(n, c - 4))
                    (sp.dma_start(tables[n][at:at + w, :].rearrange("(b p) f -> p b f", p=P), view_of(c, w))
                       .then_inc(chunk_out[c % 4], 16))

            table_halves(0)
            sweep(sp, layer0)
            sp.wait_ge(blocks_turned, NTB)
            sp.dma_start(accT[F:F + 1, 0:NPAD], accT[MUL:MUL + 1, 0:NPAD]).then_inc(counts_moved, 16)
            table_halves(1)
            sweep(sp, lambda step, first, last: [load_idx(1, step, u, first, last) for u in range(UNROLL)])
            table_chunks(2, lambda c, w: table2[:, c * CH:c * CH + w // P, :])
            sweep(sp, lambda step, first, last: [load_idx(2, step, u, first, last) for u in range(UNROLL)])
            table_chunks(3, lambda c, w: lnA[:, c * CH:c * CH + w // P, :])
            sweep(sp, lambda step, first, last: [load_idx(3, step, u, first, last) for u in range(UNROLL)])
            for k in range(NTB):
                sp.wait_ge(out_ready, k + 1)
                b0, b1_ = k * TB, (k + 1) * TB - (k == NTB - 1)
                sp.dma_start(out[b0 * P:b1_ * P, :].rearrange("(b p) f -> p b f", p=P),
                             lnA[:, b0:b1_, :]).then_inc(out_done, 16)
            sp.dma_start(out[(NB - 1) * P:N, :], lnA[0:NTAIL, NB - 1, :]).then_inc(out_done, 16)
            sp.wait_ge(out_done, 16 * (NTB + 1))

        @block.gpsimd
        def _(pool):
            nc.gpsimd.memset(xn[:, NB - 1, :], 0.0).then_inc(pads, 1)
            nc.gpsimd.memset(dst_i[:, (NG - 1) * TPG:NG * TPG], -WIN).then_inc(pads, 1)
            nc.gpsimd.memset(attr[:, (NG - 1) * TPG:NG * TPG, :], 1.0).then_inc(pads, 1)
            nc.gpsimd.iota(iota_i[:, :], pattern=[[1, WIN]], base=0, channel_multiplier=0).then_inc(made, 1)
            nc.gpsimd.iota(far_shift_i[:, :], pattern=[[WIN, NB + 1]], base=0, channel_multiplier=0).then_inc(made, 1)
            nc.gpsimd.memset(ident[:, :], 0.0).then_inc(made, 1)
            nc.gpsimd.memset(one[:, :], 1.0).then_inc(made, 1)
            nc.gpsimd.memset(ew_row[:, :, :], 0.0).then_inc(made, 1)
            nc.gpsimd.memset(idx[:, :, :], 0).then_inc(made, 1)
            pool.wait_ge(made, 6)
            nc.gpsimd.memset(hidT[HID0:HID0 + 1, :, :, :], 1.0).then_inc(made, 1)
            pool.wait_ge(made, 7)
            nc.gpsimd.affine_select(out=ident[:, :], in_=ident[:, :], compare_op=ALU.not_equal, fill=1.0,
                                    base=0, pattern=[[-1, P]], channel_multiplier=1).then_inc(made, 1)

            turn = [pool.alloc_register(f"turn_pool{u}") for u in range(UNROLL)]

            def gathers(n):
                def body(step, first, last):
                    for u in range(UNROLL):
                        pool.wait_ge(idx_in[u], step.times(16, 16 * (n * NIT + 1)))
                        free = (rows_copied if n == 0 else added)[u]
                        if last:
                            pool.wait_ge(free, NIT - 1 + n * NIT)
                        elif not first:
                            pool.wait_ge(free, pool.snap(turn[u]) + (n * NIT + 1))
                            pool.reg_add(turn[u], turn[u], 1)
                        for j in range(TTAIL if last and u == UNROLL - 1 else TPG):
                            (pool.indirect_dma_start(rows[:, u, j, 0:WIDTH[n]], None, tables[n],
                                                     bass.IndirectOffsetOnAxis(ap=idx[:, u, j:j + 1], axis=0))
                                 .then_inc(gathered[u], 16))
                    if n == 0 and first:
                        pool.wait_ge(prepared, 1)
                        nc.gpsimd.memset(accT[:, :], 0.0).then_inc(acc_cleared, 1)
                if n < 2:
                    pool.wait_ge(table_out[n], 32)
                else:
                    for c in range(NCH - 4, NCH):
                        pool.wait_ge(chunk_out[c % 4], chunks_stored(n, c))
                for u in range(UNROLL):
                    pool.reg_mov(turn[u], 0)
                sweep(pool, body)

            for n in range(NLAYER):
                gathers(n)

        @block.scalar
        def _(act):
            act.dma_start(w1c[:, :], w1.rearrange("a n -> n a")).then_inc(consts_in, 16)
            act.dma_start(b1c[:, :], b1.rearrange("(n a) -> n a", a=1)).then_inc(consts_in, 16)
            act.dma_start(w2raw[0:HID0, :], w2).then_inc(consts_in, 16)
            act.dma_start(w2raw[HID0:HID0 + 1, :], b2.rearrange("(a n) -> a n", a=1)).then_inc(consts_in, 16)
            act.dma_start(W1s[0:F, :], W1).then_inc(convs_in, 16)
            act.dma_start(W2s[:, :], W2).then_inc(convs_in, 16)
            act.dma_start(W3s[:, :], W3).then_inc(convs_in, 16)
            act.dma_start(W1s[F:F + 1, :], B1.rearrange("(a n) -> a n", a=1)).then_inc(convs_in, 16)
            act.dma_start(B2c[:, :], B2.rearrange("(n a) -> n a", a=1)).then_inc(convs_in, 16)
            act.dma_start(B3r[:, :], B3.partition_broadcast(P)).then_inc(convs_in, 16)

            def squares_of_centred(n):
                for k, bs in enumerate(HALVES):
                    act.wait_ge(centred, 2 * n + k + 1)
                    nc.scalar.activation(lnB[:, bs, :], lnA[:, bs, :], ACT.Square).then_inc(ln_squared, 1)

            def root(n, ap):
                act.wait_ge(root_asked, n)
                nc.scalar.activation(ap, ap, ACT.Sqrt).then_inc(root_done, 1)

            def make_onehot(n, step, u, first):
                if n == 0:
                    if not (first and u < 2):
                        act.wait_ge(*when(half_summed, step, 2 * (u - 2) + 1, each=2))
                elif n == 1 and first and u < 2:
                    act.wait_ge(*when(half_summed, step, 2 * (u - 2) + 1, each=2, layer=1))
                else:
                    act.wait_ge(*when(group_summed, step, u - 2, layer=n - 1))
                if n > 0 or not (first and u == 0):
                    act.wait_ge(*when(onehot_ready, step, u - 1, layer=n))
                for j in range(TPG):
                    ins = nc.scalar.activation(dist[:, j, :], iota[:, :], ACT.Abs, scale=-1.0,
                                               bias=rel[:, bass.ds(step.tile(u) + j, 1)])
                ins.then_inc(dist_ready[u % 2], 1)
                act.wait_ge(*when(dist_ready, step, u, layer=n))
                nc.scalar.activation(onehot[:, u % 2, :, :], dist[:, :, :], ACT.Relu, scale=-1.0,
                                     bias=one[:, :]).then_inc(onehot_ready[u], 1)

            def layer0(step, first, last):
                for u in range(UNROLL):
                    act.wait_ge(ew_in[u], step.times(16, 16))
                    if not (first and u < 2):
                        act.wait_ge(*when(radial_ready, step, 4 * (u - 2) + 3, each=4))
                    tail = last and u == UNROLL - 1
                    tiles, used = (TTAIL, PTAIL) if tail else (TPG, P)
                    nc.scalar.activation(hidT[0:HID0, u % 2, 0:tiles, 0:used],
                                         ew_row[:, u % 2, 0:tiles * used].rearrange("c (p j) -> c j p", j=tiles),
                                         ACT.Relu, bias=b1c[:, :], scale=w1c[:, :]).then_inc(hid_ready[u], 1)
                    act.wait_ge(gathered[u], rows_gathered(step, u, 0, 1, last))
                    if not (first and u < 2):
                        act.wait_ge(*when(prods_done, step, 4 * (u - 2) + 3, each=4))
                    vec = rows[:, u, :, MUL:F].rearrange("p t (v i) -> p t i v", i=3)
                    nc.scalar.copy(featV[:, u % 2, :, 0:3, 0:MUL], vec)
                    nc.scalar.copy(vectors[:, u % 2, :, 0:3, :], vec)
                    nc.scalar.copy(vectors[:, u % 2, :, 3:5, :], vec[:, :, 0:2, :])
                    nc.scalar.copy(featS[:, u % 2, :, 0:MUL], rows[:, u, :, 0:MUL]).then_inc(rows_copied[u], 1)
                    make_onehot(0, step, u, first)

            squares_of_centred(0)
            root(1, var[:, :])
            act.wait_ge(edges_in, 32)
            act.wait_ge(edges_tail, 32)
            nc.scalar.activation(squares, attr, ACT.Square).then_inc(squared, 1)
            root(2, length[:, :])
            act.wait_ge(directed, 1)
            nc.scalar.copy(direction[:, :, 0:2], direction[:, :, 3:5]).then_inc(repeated, 1)
            act.wait_ge(consts_in, 64)
            act.wait_ge(made, 8)
            act.wait_ge(prepared, 1)
            sweep(act, layer0)
            root(3, dis[:, :])
            squares_of_centred(1)
            root(4, var[:, :])
            def own_term(n, rows_):
                for c, at, w in chunks:
                    act.wait_ge(feat_turned, (n - 1) * NCH + c + 1)
                    nc.scalar.copy(accT[0:rows_, at:at + w], radial[1][0:rows_, c % 2, 0:w]).then_inc(acc_set, 1)

            act.wait_ge(counts_moved, 16)
            own_term(1, F)
            act.wait_ge(norm_turned, 1)
            nc.scalar.copy(norm_cols[:, :], psX[0:NB, 0:P]).then_inc(norm_copied, 1)
            act.wait_ge(norm_copied, 1)
            act.dma_start(norm_d, norm_cols[:, :]).then_inc(norm_out, 16)
            nc.scalar.activation(accT[F:F + 1, 0:NPAD], accT[F:F + 1, 0:NPAD], ACT.Sqrt,
                                 bias=one[F:F + 1, :]).then_inc(row_rooted, 1)

            def conv(n):
                sweep(act, lambda step, first, last: [make_onehot(n, step, u, first) for u in range(UNROLL)])

            conv(1)
            own_term(2, HID)
            for c in range(NCH - 4, NCH):
                act.wait_ge(chunk_out[c % 4], chunks_stored(2, c))
            act.wait_ge(norm_out, 16)
            act.dma_start(norm_row, norm_d.rearrange("b p -> (b p)").partition_broadcast(P)).then_inc(norm_in, 16)
            conv(2)
            act.wait_ge(convs_in, 96)
            for c, at, w in chunks:
                act.wait_ge(scaled, c + 1)
                if c >= 2:
                    act.wait_ge(projected, c - 1)
                nc.scalar.activation(rbuf[:, c % 2, 0:w], ybuf[:, c % 2, 0:w], ACT.Relu,
                                     bias=B2c[:, :]).then_inc(relued, 1)
            own_term(3, F)
            conv(3)

        @block.vector
        def _(dve):
            v = nc.vector
            chain = [0]

            def link(ins):
                chain[0] += 1
                ins.then_inc(v_chain, 1)
                dve.wait_ge(v_chain, chain[0])

            roots = [0]

            def reciprocal_root(ap):
                roots[0] += 1
                v.memset(flag[:, :], 0.0).then_inc(root_asked, 1)
                dve.wait_ge(root_done, roots[0])
                link(v.reciprocal(ap, ap))

            def layernorm(n, norms):
                link(v.tensor_reduce(mu[:, :], xn[:, :, :], X, ALU.add))
                link(v.tensor_scalar(mu[:, :], mu[:, :], 1.0 / F, None, ALU.mult))
                for bs in HALVES:
                    v.tensor_tensor(lnA[:, bs, :], xn[:, bs, :],
                                    mu[:, bs].unsqueeze(2).to_broadcast([P, bs.stop - bs.start, F]),
                                    ALU.subtract).then_inc(centred, 1)
                for k, bs in enumerate(HALVES):
                    dve.wait_ge(ln_squared, 2 * n + k + 1)
                    last = v.tensor_reduce(var[:, bs], lnB[:, bs, :], X, ALU.add)
                link(last)
                link(v.tensor_scalar(var[:, :], var[:, :], 1.0 / F, EPS, ALU.mult, ALU.add))
                reciprocal_root(var[:, :])
                if norms is not None:
                    link(v.tensor_tensor(var[:, :], var[:, :], norms, ALU.mult))
                dve.wait_ge(centred, 2 * n + 2)
                for bs in HALVES:
                    v.scalar_tensor_tensor(lnA[:, bs, :], lnA[:, bs, :], 0.0,
                                           var[:, bs].unsqueeze(2).to_broadcast([P, bs.stop - bs.start, F]),
                                           ALU.max, ALU.mult).then_inc(table_ready[n], 1)

            link(v.memset(nodes[:, :], 0.0))
            link(v.memset(nodesX[:, :], 0.0))
            dve.wait_ge(x_in, 16)
            dve.wait_ge(x_tail, 16)
            layernorm(0, None)

            dve.wait_ge(rows_in, 48)
            link(v.tensor_reduce(span_i[:, :, 0], dst_rows, X, ALU.min))
            link(v.tensor_reduce(span_i[:, :, 1], dst_rows, X, ALU.max))
            link(v.tensor_copy(meta_i[:, :, 0], span_i[:, :, 0]))
            link(v.tensor_tensor(span_i[:, :, 1], span_i[:, :, 1], span_i[:, :, 0], ALU.subtract))
            v.tensor_scalar(meta_i[:, :, 1], span_i[:, :, 1], WIN.bit_length() - 1, None,
                            ALU.arith_shift_right).then_inc(meta_ready, 1)
            dve.wait_ge(made, 8)
            v.tensor_copy(iota[:, :], iota_i[:, :]).then_inc(meta_ready, 1)
            link(v.tensor_copy(far_shift[:, :], far_shift_i[:, :]))
            dve.wait_ge(meta_ready, 2)
            dve.wait_ge(consts_in, 64)
            wA = w2n[:, 0:256].rearrange("k (m u g v) -> k m u g v", m=2, u=MUL, g=2)
            wB = w2n[:, 256:384].rearrange("k (u m v) -> k u m v", u=MUL, m=2)
            raw = [w2raw[:, n * 64:(n + 1) * 64].rearrange("k (u v) -> k u v", v=MUL) for n in range(3)]
            raw11 = w2raw[:, 192:384].rearrange("k (u v m) -> k u v m", u=MUL, v=MUL)
            link(v.tensor_scalar(wA[:, 1, :, 0, :], raw[0], K00, None, ALU.mult))
            link(v.tensor_scalar(wA[:, 1, :, 1, :], raw[1], K01, None, ALU.mult))
            link(v.tensor_scalar(wA[:, 0, :, 0, :], raw[2], K10, None, ALU.mult))
            link(v.tensor_scalar(wA[:, 0, :, 1, :], raw11[:, :, :, 2], K11_2, None, ALU.mult))
            link(v.tensor_scalar(wB[:, :, 1, :], raw11[:, :, :, 1], K11_1, None, ALU.mult))
            link(v.tensor_scalar(w2raw[:, 0:64], w2raw[:, 192:384].rearrange("k (n m) -> k n m", m=3)[:, :, 2],
                                 -K11_2 / 3, None, ALU.mult))
            link(v.tensor_scalar(w2raw[:, 64:128], w2raw[:, 192:384].rearrange("k (n m) -> k n m", m=3)[:, :, 0],
                                 K11_0, None, ALU.mult))
            link(v.tensor_tensor(wB[:, :, 0, :], raw[0], raw[1], ALU.add))
            dve.wait_ge(edges_in, 32)
            dve.wait_ge(edges_tail, 32)
            dve.wait_ge(meta_in, 16)
            start_all = meta[:, :].rearrange("p (g c) -> p g c", c=2)[:, :, 0:1].to_broadcast([P, NG, TPG])
            link(v.tensor_tensor(rel[:, :].rearrange("p (g j) -> p g j", j=TPG),
                                 dst_i.rearrange("p (g j) -> p g j", j=TPG), start_all, ALU.subtract))
            dve.wait_ge(squared, 1)
            link(v.tensor_reduce(length[:, :], squares, X, ALU.add))
            reciprocal_root(length[:, :])
            v.tensor_tensor(direction[:, :, 2:5], attr, length[:, :].unsqueeze(2).to_broadcast([P, NG * TPG, 3]),
                            ALU.mult).then_inc(directed, 1)
            by_group = meta[0:1, :].rearrange("p (g c) -> p g c", c=2)
            link(v.memset(late_starts[:, :], 0))
            link(v.tensor_copy(starts[:, 0:NG], by_group[:, :, 0]))
            link(v.tensor_copy(late_starts[:, 1:NG + 1], by_group[:, :, 0]))
            link(v.tensor_copy(further[:, 0:NG], by_group[:, :, 1]))
            dve.wait_ge(directed, 1)
            dve.wait_ge(table_out[0], 32)
            link(v.memset(msg[:, :, :, 16:17], 1.0))
            dve.wait_ge(repeated, 1)
            v.memset(relX[:, :], 0.0).then_inc(prepared, 1)

            far_count = dve.alloc_register("far_count")

            def far_windows(n, step, u, n_far):
                with dve.If(n_far > 0):
                    start = dve.value_load(starts[0:1, bass.ds(step.it * UNROLL + u, 1)], min_val=0, max_val=N - 1)
                    if n == 0:
                        dve.wait_ge(acc_cleared, 1)
                    with dve.Fori(1, n_far + 1) as k:
                        dve.reg_add(far_count, far_count, 1)
                        count = dve.snap(far_count)
                        v.tensor_scalar(relX[:, :], rel[:, bass.ds(step.it * (UNROLL * TPG) + u * TPG, TPG)], far_shift[:, bass.ds(k, 1)],
                                        None, ALU.subtract).then_inc(far_rel[n], 1)
                        dve.wait_ge(far_rel[n], count)
                        v.tensor_tensor(onehotX[:, :, :], iota[:, :].unsqueeze(1).to_broadcast([P, TPG, WIN]),
                                        relX[:, :].unsqueeze(2).to_broadcast([P, TPG, WIN]),
                                        ALU.is_equal).then_inc(far_onehot[n], 1)
                        dve.wait_ge(far_summed[n], count)
                        first_node = nc.s_assert_within(
                            start + k * WIN, 0, N - 1, skip_runtime_bounds_check_because=
                            "a window starts at or below its group's greatest destination")
                        at = bass.ds(first_node, WIN)
                        if n == 0:
                            v.tensor_copy(nodesX[:, 0:MUL + 1], psX[:, 0:MUL + 1])
                            v.tensor_reduce(nodesX[:, MUL + 1:F + 1],
                                            psX[:, MUL + 1:SEGW].rearrange("p (c s) -> p c s", s=16),
                                            X, ALU.add).then_inc(far_nodes, 1)
                            dve.wait_ge(far_turned, count)
                            v.tensor_tensor(accT[0:F + 1, at], accT[0:F + 1, at], psT[0:F + 1, 0:WIN],
                                            ALU.add).then_inc(far_added[n], 1)
                        else:
                            w = WIDTH[n]
                            v.tensor_tensor(accT[0:w, at], accT[0:w, at], psX[0:w, 0:WIN],
                                            ALU.add).then_inc(far_added[n], 1)
                        dve.wait_ge(far_added[n], count)

            shapeV = [P, TPG, 3, MUL]

            def along_parts(step, u):
                s, d = u % 2, direction[:, bass.ds(step.tile(u), TPG), :]
                dve.wait_ge(*when(rows_copied, step, u))
                v.tensor_tensor(dotp[:, :, :, :], vectors[:, s, :, 0:3, :],
                                d[:, :, 0:3].unsqueeze(3).to_broadcast(shapeV), ALU.mult).then_inc(dot_ready[u % 2], 1)

            def cross_parts(step, u):
                s, d = u % 2, direction[:, bass.ds(step.tile(u), TPG), :]
                v.tensor_tensor(cross1[:, :, :, :], vectors[:, s, :, 2:5, :],
                                d[:, :, 1:4].unsqueeze(3).to_broadcast(shapeV), ALU.mult)
                v.tensor_tensor(cross2[:, :, :, :], vectors[:, s, :, 1:4, :],
                                d[:, :, 2:5].unsqueeze(3).to_broadcast(shapeV), ALU.mult).then_inc(cross_ready[u % 2], 1)

            def feature_along(step, u):
                dve.wait_ge(*when(dot_ready, step, u))
                v.tensor_reduce(featS[:, u % 2, :, MUL:2 * MUL],
                                dotp[:, :, :, :].rearrange("p t i v -> p t v i"),
                                X, ALU.add).then_inc(feat_along_ready[u % 2], 1)

            def feature_cross(step, u):
                dve.wait_ge(*when(cross_ready, step, u))
                v.tensor_tensor(featV[:, u % 2, :, 0:3, MUL:2 * MUL], cross1[:, :, :, :], cross2[:, :, :, :],
                                ALU.subtract).then_inc(feats_ready[u % 2], 1)

            def products(step, u, h, first):
                s = u % 2
                if not (first and u == 0):
                    dve.wait_ge(*when(half_summed, step, 2 * (u - 1) + h, each=2))
                for q in range(2):
                    dve.wait_ge(*when(radial_ready, step, 4 * u + 2 * h + q, each=4))
                    if h == 0 and q == 0:
                        dve.wait_ge(*when(feat_along_ready, step, u))
                    R = radial[q]
                    t = 2 * q
                    prod = v.tensor_tensor(
                        prodA[:, h, t:t + 2, :].rearrange("p t (m s) -> p t m s", s=16),
                        R[:, :, 0:256].rearrange("p t (m s) -> p t m s", s=16),
                        featS[:, s, 4 * h + t:4 * h + t + 2, :].unsqueeze(2).to_broadcast([P, 2, 16, 16]), ALU.mult)
                    if q == 1:
                        prod.then_inc(scalar_prods[(2 * u + h) % 4], 1)
                    elif h == 0:
                        dve.wait_ge(*when(feats_ready, step, u))
                    last = v.tensor_tensor(
                        msg[:, h, t:t + 2, 17:401].rearrange("p t (i u s) -> p t i (u s)", i=3, u=MUL),
                        R[:, :, 256:384].unsqueeze(2).to_broadcast([P, 2, 3, 128]),
                        featV[:, s, 4 * h + t:4 * h + t + 2, :, :].rearrange("p t i s -> p (t i) s").unsqueeze(2)
                        .to_broadcast([P, 6, MUL, 16]), ALU.mult)
                    last.then_inc(prods_done[(4 * u + 2 * h + q) % 8], 1)

            def scalar_sums(step, u, h):
                dve.wait_ge(*when(scalar_prods, step, 2 * u + h, each=2))
                v.tensor_reduce(msg[:, h, :, 0:16], prodA[:, h, :, :].rearrange("p t (m s) -> p t m s", s=16),
                                X, ALU.add).then_inc(scalars_ready[(2 * u + h) % 4], 1)

            def direction_part(step, u, h):
                dve.wait_ge(*when(scalars_ready, step, 2 * u + h, each=2))
                v.tensor_tensor(along[:, :, :, :], msg[:, h, :, 0:MUL].unsqueeze(2).to_broadcast([P, 4, 3, MUL]),
                                direction[:, bass.ds(step.tile(u) + 4 * h, 4), 0:3].unsqueeze(3)
                                .to_broadcast([P, 4, 3, MUL]),
                                ALU.mult).then_inc(along_ready[(2 * u + h) % 4], 1)

            def add_direction_part(step, u, h):
                dve.wait_ge(*when(along_ready, step, 2 * u + h, each=2))
                slot = msg[:, h, :, 17:401].rearrange("p t (n s) -> p t n s", s=16)[:, :, :, 0]
                v.tensor_tensor(slot, slot, along[:, :, :, :].rearrange("p t o u -> p t (o u)"),
                                ALU.add).then_inc(msg_ready[(2 * u + h) % 4], 1)

            def window_sums(step, u):
                dve.wait_ge(*when(half_summed, step, 2 * u + 1, each=2))
                v.tensor_copy(nodes[:, 0:MUL + 1], sums[:, u % 2, 0:MUL + 1])
                v.tensor_reduce(nodes[:, MUL + 1:F + 1],
                                sums[:, u % 2, MUL + 1:SEGW].rearrange("p (c s) -> p c s", s=16),
                                X, ALU.add).then_inc(nodes_ready[u % UNROLL], 1)

            def window_add(step, u, start, first):
                dve.wait_ge(*when(nodes_turned, step, u))
                if not (first and u == 0):
                    dve.wait_ge(*when(added, step, u - 1))
                window = bass.ds(start, WIN)
                v.tensor_tensor(accT[0:F + 1, window], accT[0:F + 1, window], psT[0:F + 1, 0:WIN],
                                ALU.add).then_inc(added[u % UNROLL], 1)

            def load_registers(table, step, top):
                return nc.values_load_multi_w_load_instructions(
                    table[0:1, bass.ds(step.times(UNROLL, 0), UNROLL)], [dve.engine], min_val=0, max_val=top,
                    skip_runtime_bounds_check_because=IN_RANGE)[1]

            def layer0(step, first, last):
                for u in range(UNROLL):
                    before = not (first and u == 0)
                    after = not (last and u == UNROLL - 1)
                    products(step, u, 0, first)
                    if u == 0:
                        late_start = load_registers(late_starts, step, N - 1)
                        n_far = load_registers(further, step, NB)
                    scalar_sums(step, u, 0)
                    if before:
                        window_sums(step, u - 1)
                    direction_part(step, u, 0)
                    if after:
                        along_parts(step, u + 1)
                    add_direction_part(step, u, 0)
                    products(step, u, 1, first)
                    scalar_sums(step, u, 1)
                    if after:
                        cross_parts(step, u + 1)
                    direction_part(step, u, 1)
                    if before:
                        if first and u == 1:
                            dve.wait_ge(acc_cleared, 1)
                        window_add(step, u - 1, late_start[u], first)
                    add_direction_part(step, u, 1)
                    if after:
                        feature_along(step, u + 1)
                    far_windows(0, step, u, n_far[u])
                    if after:
                        feature_cross(step, u + 1)

            dve.reg_mov(far_count, 0)
            along_parts(first_step, 0)
            cross_parts(first_step, 0)
            feature_along(first_step, 0)
            feature_cross(first_step, 0)
            sweep(dve, layer0)
            window_sums(last_step, UNROLL - 1)
            window_add(last_step, UNROLL - 1,
                       dve.value_load(starts[0:1, NG - 1:NG], min_val=0, max_val=N - 1), False)

            for k in range(NTB):
                dve.wait_ge(blocks_turned, k + 1)
                bs = slice(k * TB, (k + 1) * TB)
                ps = radial[0][:, k % 2, 0:TB * (F + 1)].rearrange("p (b c) -> p b c", c=F + 1)
                v.tensor_tensor(xn[:, bs, 0:MUL], xn[:, bs, 0:MUL], ps[:, :, 0:MUL], ALU.add)
                xv = xn[:, bs, MUL:F].rearrange("p b (u o) -> p b o u", o=3)
                v.tensor_tensor(xv, xv, ps[:, :, MUL + 1:F + 1].rearrange("p b (o u) -> p b o u", o=3), ALU.add)
                v.tensor_scalar(dis[:, bs], ps[:, :, MUL], 1.0, None, ALU.add).then_inc(blocks_read, 1)
            dve.wait_ge(blocks_read, NTB)
            reciprocal_root(dis[:, :])
            layernorm(1, dis[:, :])
            link(v.tensor_tensor(dis2[:, :], dis[:, :], dis[:, :], ALU.mult))

            def conv(n):
                w = WIDTH[n]

                def body(step, first, last):
                    start = load_registers(starts, step, N - 1)
                    n_far = load_registers(further, step, NB)
                    for u in range(UNROLL):
                        far_windows(n, step, u, n_far[u])
                        dve.wait_ge(*when(group_summed, step, u, layer=n - 1))
                        dve.wait_ge(*when(added, step, u - 1, layer=n))
                        window = bass.ds(start[u], WIN)
                        v.tensor_tensor(accT[0:w, window], accT[0:w, window], sums[0:w, u % 2, 0:WIN],
                                        ALU.add).then_inc(added[u], 1)
                dve.reg_mov(far_count, 0)
                sweep(dve, body)

            def table_after_first():
                for c, at, w in chunks:
                    dve.wait_ge(weighed[0], c + 1)
                    b = w // P
                    v.scalar_tensor_tensor(table2[:, c * CH:c * CH + b, :],
                                           radial[0][:, c % 2, 0:w].rearrange("p (b f) -> p b f", f=HID), 0.0,
                                           dis2[:, c * CH:c * CH + b].unsqueeze(2).to_broadcast([P, b, HID]),
                                           ALU.max, ALU.mult).then_inc(next_set[0], 1)

            def table_after_second():
                def scale(c, at, w):
                    dve.wait_ge(weighed[1], c + 1)
                    if c >= 2:
                        dve.wait_ge(relued, c - 1)
                    v.tensor_tensor(ybuf[:, c % 2, 0:w], radial[0][:, c % 2, 0:w], norm_row[:, at:at + w],
                                    ALU.mult).then_inc(scaled, 1)

                def table_chunk(c, at, w):
                    b = w // P
                    dve.wait_ge(projected, c + 1)
                    v.tensor_tensor(lnA[:, c * CH:c * CH + b, :],
                                    sums[:, c % 2, 0:b * F].rearrange("p (b f) -> p b f", f=F),
                                    dis[:, c * CH:c * CH + b].unsqueeze(2).to_broadcast([P, b, F]),
                                    ALU.mult).then_inc(next_set[1], 1)

                for c in range(NCH + 2):
                    if c < NCH:
                        scale(*chunks[c])
                    if c >= 2:
                        table_chunk(*chunks[c - 2])

            dve.wait_ge(acc_set, NCH)
            conv(1)
            table_after_first()
            dve.wait_ge(acc_set, 2 * NCH)
            conv(2)
            dve.wait_ge(norm_in, 16)
            table_after_second()
            dve.wait_ge(acc_set, 3 * NCH)
            conv(3)

            dve.wait_ge(convs_in, 96)
            for k in range(NTB):
                dve.wait_ge(out_turned, k + 1)
                bs = slice(k * TB, (k + 1) * TB)
                ps = radial[0][:, k % 2, 0:TB * F].rearrange("p (b c) -> p b c", c=F)
                link(v.tensor_tensor(lnA[:, bs, :], ps, dis[:, bs].unsqueeze(2).to_broadcast([P, TB, F]), ALU.mult))
                link(v.tensor_tensor(lnA[:, bs, :], lnA[:, bs, :], B3r[:, :].unsqueeze(1).to_broadcast([P, TB, F]),
                                     ALU.add))
                v.scalar_tensor_tensor(lnA[:, bs, :], lnA[:, bs, :], 0.0, xn[:, bs, :],
                                       ALU.max, ALU.add).then_inc(out_ready, 1)

        @block.tensor
        def _(pe):
            far_count = pe.alloc_register("far_count_pe")
            turn = [pe.alloc_register(f"turn_pe{u}") for u in range(UNROLL)]

            def load_further(step):
                return nc.values_load_multi_w_load_instructions(
                    further[0:1, bass.ds(step.times(UNROLL, 0), UNROLL)], [pe.engine], min_val=0, max_val=NB,
                    skip_runtime_bounds_check_because=IN_RANGE)[1]

            def far_windows(n, n_far):
                with pe.If(n_far > 0):
                    with pe.Fori(1, n_far + 1):
                        count = pe.snap(far_count) + 1
                        pe.wait_ge(far_onehot[n], count)
                        for j in range(TPG):
                            if n == 0:
                                last = nc.tensor.matmul(psX[:, 0:SEGW], onehotX[:, j, :],
                                                        msg[:, j // 4, j % 4, MUL:MUL + SEGW],
                                                        start=(j == 0), stop=(j == TPG - 1))
                            else:
                                last = nc.tensor.matmul(psX[0:WIDTH[n], 0:WIN], far_rows[j], onehotX[:, j, :],
                                                        start=(j == 0), stop=(j == TPG - 1))
                        last.then_inc(far_summed[n], 1)
                        if n == 0:
                            pe.wait_ge(far_nodes, count)
                            pe.reg_add(far_count, far_count, 1)
                            nc.tensor.transpose(psT[0:F + 1, 0:P], nodesX[:, :], ident[:, :]).then_inc(far_turned, 1)
                        else:
                            pe.reg_add(far_count, far_count, 1)

            def radial_pair(step, u, q, free=True):
                if q == 0:
                    pe.wait_ge(*when(hid_ready, step, u))
                if free:
                    pe.wait_ge(*when(prods_done, step, 4 * u + q - 2, each=4))
                for k in range(2):
                    last = nc.tensor.matmul(radial[q % 2][:, k, 0:RDIM], hidT[:, u % 2, 2 * q + k, :], w2n[:, :],
                                            start=True, stop=True)
                last.then_inc(radial_ready[(4 * u + q) % 8], 1)

            def sum_half(step, u, h, first):
                pe.wait_ge(*when(msg_ready, step, 2 * u + h, each=2))
                if h == 0:
                    pe.wait_ge(*when(onehot_ready, step, u))
                    if not (first and u < 2):
                        pe.wait_ge(*when(nodes_ready, step, u - 2))
                for k in range(4):
                    last = nc.tensor.matmul(sums[:, u % 2, 0:SEGW], onehot[:, u % 2, 4 * h + k, :],
                                            msg[:, h, k, MUL:MUL + SEGW],
                                            start=(h == 0 and k == 0), stop=(h == 1 and k == 3))
                last.then_inc(half_summed[(2 * u + h) % 4], 1)

            def turn_nodes(step, u, first):
                r = u % UNROLL
                now = step.it if step.peeled else pe.snap(turn[r]) + 1
                pe.wait_ge(nodes_ready[r], now + (1 if u >= 0 else 0))
                if not (first and u == 0):
                    pe.wait_ge(*when(added, step, u - 1))
                if not step.peeled:
                    pe.reg_add(turn[r], turn[r], 1)
                nc.tensor.transpose(psT[0:F + 1, 0:P], nodes[:, :], ident[:, :]).then_inc(nodes_turned[r], 1)

            def layer0(step, first, last):
                for u in range(UNROLL):
                    radial_pair(step, u, 2)
                    if u == 0:
                        n_far = load_further(step)
                    radial_pair(step, u, 3)
                    sum_half(step, u, 0, first)
                    if not (first and u == 0):
                        turn_nodes(step, u - 1, first)
                    if not (last and u == UNROLL - 1):
                        radial_pair(step, u + 1, 0)
                        radial_pair(step, u + 1, 1)
                    sum_half(step, u, 1, first)
                    far_windows(0, n_far[u])

            pe.wait_ge(made, 8)
            pe.wait_ge(prepared, 1)
            pe.wait_ge(meta_in, 16)
            pe.reg_mov(far_count, 0)
            for u in range(UNROLL):
                pe.reg_mov(turn[u], 0)
            radial_pair(first_step, 0, 0, False)
            radial_pair(first_step, 0, 1, False)
            sweep(pe, layer0)
            turn_nodes(last_step, UNROLL - 1, False)

            pe.wait_ge(*when(added, last_step, UNROLL - 1))
            for k in range(NTB):
                if k >= 2:
                    pe.wait_ge(blocks_read, k - 1)
                for j in range(TB):
                    at = (k * TB + j) * P
                    last = nc.tensor.transpose(radial[0][:, k % 2, j * (F + 1):(j + 1) * (F + 1)],
                                               accT[0:F + 1, at:at + P], ident[0:F + 1, 0:F + 1])
                last.then_inc(blocks_turned, 1)
            def turn_chunk(n, c, w, view):
                count = (n - 1) * NCH + c
                if count >= 2:
                    pe.wait_ge(acc_set, count - 1)
                for j in range(w // P):
                    last = nc.tensor.transpose(radial[1][0:WIDTH[n], c % 2, j * P:(j + 1) * P], view(j), ident[:, :])
                last.then_inc(feat_turned, 1)

            pe.wait_ge(table_ready[1], 2)
            for c, at, w in chunks:
                turn_chunk(1, c, w, lambda j: lnA[:, c * CH + j, :])
            nc.tensor.transpose(psX[0:NB, 0:P], dis[:, :], ident[:, :]).then_inc(norm_turned, 1)

            def conv(n):
                w = WIDTH[n]

                def body(step, first, last):
                    n_far = load_further(step)
                    for u in range(UNROLL):
                        pe.wait_ge(gathered[u], rows_gathered(step, u, n, 1, last))
                        pe.wait_ge(*when(onehot_ready, step, u, layer=n))
                        pe.wait_ge(*when(added, step, u - 2, layer=n))
                        for j in range(TPG):
                            mm = nc.tensor.matmul(sums[0:w, u % 2, 0:WIN], rows[:, u, j, 0:w],
                                                  onehot[:, u % 2, j, :], start=(j == 0), stop=(j == TPG - 1))
                        mm.then_inc(group_summed[u], 1)
                        for j in range(TPG):
                            far_rows[j] = rows[:, u, j, 0:w]
                        far_windows(n, n_far[u])
                pe.reg_mov(far_count, 0)
                sweep(pe, body)

            def table_after_first():
                pe.wait_ge(*when(added, last_step, UNROLL - 1, layer=1))
                pe.wait_ge(row_rooted, 1)
                for c, at, w in chunks:
                    if c >= 2:
                        pe.wait_ge(next_set[0], c - 1)
                    for j in range(w // P):
                        last = nc.tensor.matmul(radial[0][:, c % 2, j * P:(j + 1) * P],
                                                accT[0:F + 1, at + j * P:at + (j + 1) * P], W1s[:, :],
                                                start=True, stop=True)
                    last.then_inc(weighed[0], 1)
                pe.wait_ge(next_set[0], NCH)
                for c, at, w in chunks:
                    turn_chunk(2, c, w, lambda j: table2[:, c * CH + j, :])

            def table_after_second():
                def weigh(c, at, w):
                    if c >= 2:
                        pe.wait_ge(scaled, c - 1)
                    nc.tensor.matmul(radial[0][:, c % 2, 0:w], W2s[:, :], accT[:, at:at + w],
                                     start=True, stop=True).then_inc(weighed[1], 1)

                def project(c, at, w):
                    pe.wait_ge(relued, c + 1)
                    if c >= 2:
                        pe.wait_ge(next_set[1], c - 1)
                    for j in range(w // P):
                        last = nc.tensor.matmul(sums[:, c % 2, j * F:(j + 1) * F], rbuf[:, c % 2, j * P:(j + 1) * P],
                                                W3s[:, :], start=True, stop=True)
                    last.then_inc(projected, 1)

                pe.wait_ge(*when(added, last_step, UNROLL - 1, layer=2))
                for c in range(NCH + 1):
                    if c < NCH:
                        weigh(*chunks[c])
                    if c >= 1:
                        project(*chunks[c - 1])
                pe.wait_ge(next_set[1], NCH)
                for c, at, w in chunks:
                    turn_chunk(3, c, w, lambda j: lnA[:, c * CH + j, :])

            far_rows = [None] * TPG
            conv(1)
            pe.wait_ge(convs_in, 96)
            table_after_first()
            conv(2)
            table_after_second()
            conv(3)
            pe.wait_ge(*when(added, last_step, UNROLL - 1, layer=NLAYER - 1))
            for k in range(NTB):
                if k >= 2:
                    pe.wait_ge(out_ready, k - 1)
                for j in range(TB):
                    at = (k * TB + j) * P
                    last = nc.tensor.transpose(radial[0][:, k % 2, j * F:(j + 1) * F],
                                               accT[0:F, at:at + P], ident[0:F, 0:F])
                last.then_inc(out_turned, 1)


_INS = ["x", "src", "dst", "edge_attr_3", "edge_weight", "L0_gnn_w1", "L0_gnn_b1", "L0_gnn_w2", "L0_gnn_b2",
        "L1_gnn_W1", "L1_gnn_b1", "L1_gnn_W2", "L1_gnn_b2", "L1_gnn_W3", "L1_gnn_b3"]


def kernel(**inputs):
    import numpy as np
    import concourse.bacc as bacc
    from concourse.bass_utils import run_bass_kernel_spmd

    nc = bacc.Bacc("TRN2", target_bir_lowering=False, num_devices=1)
    arrays, args = {}, []
    for name in _INS:
        a = np.ascontiguousarray(inputs[name])
        arrays[f"in_{name}"] = a
        args.append(nc.dram_tensor(f"in_{name}", a.shape, mybir.dt.from_np(a.dtype), kind="ExternalInput").ap())
    args.append(nc.dram_tensor("out", (N, F), fp32, kind="ExternalOutput").ap())
    gnn_kernel(nc, *args)
    r = run_bass_kernel_spmd(nc, [arrays], core_ids=[0])
    return r.results[0]["out"]
```
